# Optimizing a Trainium2 kernel written in Bass

```python
import numpy as np
import jax
import jax.numpy as jnp

def _softmax(x, axis=-1):
    return jax.nn.softmax(x, axis=axis)

def _gelu(x):
    return jax.nn.gelu(x, approximate=True)

def _silu(x):
    return jax.nn.silu(x)

def _sigmoid(x):
    return jax.nn.sigmoid(x)

def _layernorm(x, axis=-1, eps=1e-05):
    m = jnp.mean(x, axis=axis, keepdims=True)
    v = jnp.var(x, axis=axis, keepdims=True)
    return (x - m) / jnp.sqrt(v + eps)

def _scatter_add(tgt, idx, src, axis=0):
    return tgt.at[idx].add(src)

def _segment_sum(src, seg, n):
    return jax.ops.segment_sum(src, seg, n)
kernel_name = 'mk_dlrm_tower_d1_rec_r8_3a6445'

def setup_inputs(seed: int=0):
    np.random.seed(seed)
    _w = jnp.asarray

    def _rec_inputs():
        import jax
        import jax.numpy as jnp
        _tk = jax.random.key(seed)
        dense_ctx = jax.random.normal(jax.random.fold_in(_tk, 190), (512, 16), jnp.float32)
        ids = jnp.stack([jax.random.randint(jax.random.fold_in(_tk, 200 + f), (512,), 0, v, jnp.int32) for f, v in enumerate([1250, 1250, 12500, 1250, 125000, 1250, 1250, 12500, 125000, 1250, 125000, 1000, 1000, 125000, 1000, 125000, 1250, 1250, 1250, 125000, 1250, 1250, 12500, 12500, 12500, 12500, 125000, 125000, 1000, 1000, 1250, 125000, 125000, 12500, 1250, 125000, 1000, 12500, 1250])], axis=1)
        tbl_0 = 0.05 * jax.random.normal(jax.random.fold_in(_tk, 500 + 0), (1250, 16), jnp.float32)
        tbl_1 = 0.05 * jax.random.normal(jax.random.fold_in(_tk, 500 + 1), (1250, 16), jnp.float32)
        tbl_2 = 0.05 * jax.random.normal(jax.random.fold_in(_tk, 500 + 2), (12500, 16), jnp.float32)
        tbl_3 = 0.05 * jax.random.normal(jax.random.fold_in(_tk, 500 + 3), (1250, 16), jnp.float32)
        tbl_4 = 0.05 * jax.random.normal(jax.random.fold_in(_tk, 500 + 4), (125000, 16), jnp.float32)
        tbl_5 = 0.05 * jax.random.normal(jax.random.fold_in(_tk, 500 + 5), (1250, 16), jnp.float32)
        tbl_6 = 0.05 * jax.random.normal(jax.random.fold_in(_tk, 500 + 6), (1250, 16), jnp.float32)
        tbl_7 = 0.05 * jax.random.normal(jax.random.fold_in(_tk, 500 + 7), (12500, 16), jnp.float32)
        tbl_8 = 0.05 * jax.random.normal(jax.random.fold_in(_tk, 500 + 8), (125000, 16), jnp.float32)
        tbl_9 = 0.05 * jax.random.normal(jax.random.fold_in(_tk, 500 + 9), (1250, 16), jnp.float32)
        tbl_10 = 0.05 * jax.random.normal(jax.random.fold_in(_tk, 500 + 10), (125000, 16), jnp.float32)
        tbl_11 = 0.05 * jax.random.normal(jax.random.fold_in(_tk, 500 + 11), (1000, 16), jnp.float32)
        tbl_12 = 0.05 * jax.random.normal(jax.random.fold_in(_tk, 500 + 12), (1000, 16), jnp.float32)
        tbl_13 = 0.05 * jax.random.normal(jax.random.fold_in(_tk, 500 + 13), (125000, 16), jnp.float32)
        tbl_14 = 0.05 * jax.random.normal(jax.random.fold_in(_tk, 500 + 14), (1000, 16), jnp.float32)
        tbl_15 = 0.05 * jax.random.normal(jax.random.fold_in(_tk, 500 + 15), (125000, 16), jnp.float32)
        tbl_16 = 0.05 * jax.random.normal(jax.random.fold_in(_tk, 500 + 16), (1250, 16), jnp.float32)
        tbl_17 = 0.05 * jax.random.normal(jax.random.fold_in(_tk, 500 + 17), (1250, 16), jnp.float32)
        tbl_18 = 0.05 * jax.random.normal(jax.random.fold_in(_tk, 500 + 18), (1250, 16), jnp.float32)
        tbl_19 = 0.05 * jax.random.normal(jax.random.fold_in(_tk, 500 + 19), (125000, 16), jnp.float32)
        tbl_20 = 0.05 * jax.random.normal(jax.random.fold_in(_tk, 500 + 20), (1250, 16), jnp.float32)
        tbl_21 = 0.05 * jax.random.normal(jax.random.fold_in(_tk, 500 + 21), (1250, 16), jnp.float32)
        tbl_22 = 0.05 * jax.random.normal(jax.random.fold_in(_tk, 500 + 22), (12500, 16), jnp.float32)
        tbl_23 = 0.05 * jax.random.normal(jax.random.fold_in(_tk, 500 + 23), (12500, 16), jnp.float32)
        tbl_24 = 0.05 * jax.random.normal(jax.random.fold_in(_tk, 500 + 24), (12500, 16), jnp.float32)
        tbl_25 = 0.05 * jax.random.normal(jax.random.fold_in(_tk, 500 + 25), (12500, 16), jnp.float32)
        tbl_26 = 0.05 * jax.random.normal(jax.random.fold_in(_tk, 500 + 26), (125000, 16), jnp.float32)
        tbl_27 = 0.05 * jax.random.normal(jax.random.fold_in(_tk, 500 + 27), (125000, 16), jnp.float32)
        tbl_28 = 0.05 * jax.random.normal(jax.random.fold_in(_tk, 500 + 28), (1000, 16), jnp.float32)
        tbl_29 = 0.05 * jax.random.normal(jax.random.fold_in(_tk, 500 + 29), (1000, 16), jnp.float32)
        tbl_30 = 0.05 * jax.random.normal(jax.random.fold_in(_tk, 500 + 30), (1250, 16), jnp.float32)
        tbl_31 = 0.05 * jax.random.normal(jax.random.fold_in(_tk, 500 + 31), (125000, 16), jnp.float32)
        tbl_32 = 0.05 * jax.random.normal(jax.random.fold_in(_tk, 500 + 32), (125000, 16), jnp.float32)
        tbl_33 = 0.05 * jax.random.normal(jax.random.fold_in(_tk, 500 + 33), (12500, 16), jnp.float32)
        tbl_34 = 0.05 * jax.random.normal(jax.random.fold_in(_tk, 500 + 34), (1250, 16), jnp.float32)
        tbl_35 = 0.05 * jax.random.normal(jax.random.fold_in(_tk, 500 + 35), (125000, 16), jnp.float32)
        tbl_36 = 0.05 * jax.random.normal(jax.random.fold_in(_tk, 500 + 36), (1000, 16), jnp.float32)
        tbl_37 = 0.05 * jax.random.normal(jax.random.fold_in(_tk, 500 + 37), (12500, 16), jnp.float32)
        tbl_38 = 0.05 * jax.random.normal(jax.random.fold_in(_tk, 500 + 38), (1250, 16), jnp.float32)
        _rk = jax.random.fold_in(_tk, 7)
        W_top1 = 0.0606339 * jax.random.normal(jax.random.fold_in(_tk, 801), (272, 512), jnp.float32)
        W_top2 = 0.0441942 * jax.random.normal(jax.random.fold_in(_tk, 802), (512, 256), jnp.float32)
        W_top3 = 0.0625 * jax.random.normal(jax.random.fold_in(_tk, 803), (256, 1), jnp.float32)
        b_top1 = jnp.zeros((512,), jnp.float32)
        b_top2 = jnp.zeros((256,), jnp.float32)
        return (dense_ctx, ids, tbl_0, tbl_1, tbl_2, tbl_3, tbl_4, tbl_5, tbl_6, tbl_7, tbl_8, tbl_9, tbl_10, tbl_11, tbl_12, tbl_13, tbl_14, tbl_15, tbl_16, tbl_17, tbl_18, tbl_19, tbl_20, tbl_21, tbl_22, tbl_23, tbl_24, tbl_25, tbl_26, tbl_27, tbl_28, tbl_29, tbl_30, tbl_31, tbl_32, tbl_33, tbl_34, tbl_35, tbl_36, tbl_37, tbl_38, W_top1, b_top1, W_top2, b_top2, W_top3)
    dense_ctx, ids, tbl_0, tbl_1, tbl_2, tbl_3, tbl_4, tbl_5, tbl_6, tbl_7, tbl_8, tbl_9, tbl_10, tbl_11, tbl_12, tbl_13, tbl_14, tbl_15, tbl_16, tbl_17, tbl_18, tbl_19, tbl_20, tbl_21, tbl_22, tbl_23, tbl_24, tbl_25, tbl_26, tbl_27, tbl_28, tbl_29, tbl_30, tbl_31, tbl_32, tbl_33, tbl_34, tbl_35, tbl_36, tbl_37, tbl_38, W_top1, b_top1, W_top2, b_top2, W_top3 = _rec_inputs()

    def _L0_rec_setup():
        import jax, jax.numpy as jnp
        import numpy as np
        B, M, D = (1024, 39, 16)
        S1, S2 = (128, 128)

        def _cin_layer(x0, xk, W, b):
            out = jnp.einsum('bhd,bmd,shm->bsd', xk, x0, W) + b[None, :, None]
            return jax.nn.relu(out)
        key = jax.random.key(seed)
        k0, k1, k2 = jax.random.split(key, 3)
        x0 = jax.random.normal(k0, (B, M, D), dtype=jnp.float32)
        W1 = jax.random.normal(k1, (S1, M, M), dtype=jnp.float32) * 0.05
        b1 = jnp.zeros((S1,), dtype=jnp.float32)
        W2 = jax.random.normal(k2, (S2, S1, M), dtype=jnp.float32) * 0.05
        b2 = jnp.zeros((S2,), dtype=jnp.float32)
        return {'x0': x0, 'W1': W1, 'b1': b1, 'W2': W2, 'b2': b2}
    _L0_rec_all = _L0_rec_setup()
    _L0_rec_in = {k: v for k, v in _L0_rec_all.items() if k in ('W1', 'b1', 'W2', 'b2')}
    del _L0_rec_all
    return {'dense_ctx': dense_ctx, 'ids': ids, 'tbl_0': tbl_0, 'tbl_1': tbl_1, 'tbl_2': tbl_2, 'tbl_3': tbl_3, 'tbl_4': tbl_4, 'tbl_5': tbl_5, 'tbl_6': tbl_6, 'tbl_7': tbl_7, 'tbl_8': tbl_8, 'tbl_9': tbl_9, 'tbl_10': tbl_10, 'tbl_11': tbl_11, 'tbl_12': tbl_12, 'tbl_13': tbl_13, 'tbl_14': tbl_14, 'tbl_15': tbl_15, 'tbl_16': tbl_16, 'tbl_17': tbl_17, 'tbl_18': tbl_18, 'tbl_19': tbl_19, 'tbl_20': tbl_20, 'tbl_21': tbl_21, 'tbl_22': tbl_22, 'tbl_23': tbl_23, 'tbl_24': tbl_24, 'tbl_25': tbl_25, 'tbl_26': tbl_26, 'tbl_27': tbl_27, 'tbl_28': tbl_28, 'tbl_29': tbl_29, 'tbl_30': tbl_30, 'tbl_31': tbl_31, 'tbl_32': tbl_32, 'tbl_33': tbl_33, 'tbl_34': tbl_34, 'tbl_35': tbl_35, 'tbl_36': tbl_36, 'tbl_37': tbl_37, 'tbl_38': tbl_38, 'W_top1': W_top1, 'b_top1': b_top1, 'W_top2': W_top2, 'b_top2': b_top2, 'W_top3': W_top3, 'L0_rec_W1': _L0_rec_in['W1'], 'L0_rec_b1': _L0_rec_in['b1'], 'L0_rec_W2': _L0_rec_in['W2'], 'L0_rec_b2': _L0_rec_in['b2']}

def reference(dense_ctx, ids, tbl_0, tbl_1, tbl_2, tbl_3, tbl_4, tbl_5, tbl_6, tbl_7, tbl_8, tbl_9, tbl_10, tbl_11, tbl_12, tbl_13, tbl_14, tbl_15, tbl_16, tbl_17, tbl_18, tbl_19, tbl_20, tbl_21, tbl_22, tbl_23, tbl_24, tbl_25, tbl_26, tbl_27, tbl_28, tbl_29, tbl_30, tbl_31, tbl_32, tbl_33, tbl_34, tbl_35, tbl_36, tbl_37, tbl_38, W_top1, b_top1, W_top2, b_top2, W_top3, L0_rec_W1, L0_rec_b1, L0_rec_W2, L0_rec_b2):
    import jax
    import jax.numpy as jnp

    def _L0_rec_ref(x0, W1, b1, W2, b2):
        import jax, jax.numpy as jnp
        import numpy as np
        B, M, D = (1024, 39, 16)
        S1, S2 = (128, 128)

        def _cin_layer(x0, xk, W, b):
            out = jnp.einsum('bhd,bmd,shm->bsd', xk, x0, W) + b[None, :, None]
            return jax.nn.relu(out)
        x1 = _cin_layer(x0, x0, W1, b1)
        x2 = _cin_layer(x0, x1, W2, b2)
        p1 = x1.sum(axis=-1)
        p2 = x2.sum(axis=-1)
        return jnp.concatenate([p1, p2], axis=-1)
    e = jnp.stack([tbl_0[ids[:, 0]], tbl_1[ids[:, 1]], tbl_2[ids[:, 2]], tbl_3[ids[:, 3]], tbl_4[ids[:, 4]], tbl_5[ids[:, 5]], tbl_6[ids[:, 6]], tbl_7[ids[:, 7]], tbl_8[ids[:, 8]], tbl_9[ids[:, 9]], tbl_10[ids[:, 10]], tbl_11[ids[:, 11]], tbl_12[ids[:, 12]], tbl_13[ids[:, 13]], tbl_14[ids[:, 14]], tbl_15[ids[:, 15]], tbl_16[ids[:, 16]], tbl_17[ids[:, 17]], tbl_18[ids[:, 18]], tbl_19[ids[:, 19]], tbl_20[ids[:, 20]], tbl_21[ids[:, 21]], tbl_22[ids[:, 22]], tbl_23[ids[:, 23]], tbl_24[ids[:, 24]], tbl_25[ids[:, 25]], tbl_26[ids[:, 26]], tbl_27[ids[:, 27]], tbl_28[ids[:, 28]], tbl_29[ids[:, 29]], tbl_30[ids[:, 30]], tbl_31[ids[:, 31]], tbl_32[ids[:, 32]], tbl_33[ids[:, 33]], tbl_34[ids[:, 34]], tbl_35[ids[:, 35]], tbl_36[ids[:, 36]], tbl_37[ids[:, 37]], tbl_38[ids[:, 38]]], axis=1)
    z = _L0_rec_ref(e, L0_rec_W1, L0_rec_b1, L0_rec_W2, L0_rec_b2)
    z = z.reshape(z.shape[0], -1)
    h = jnp.concatenate([z, dense_ctx], axis=1)
    h = jnp.maximum(h @ W_top1 + b_top1, 0.0)
    h = jnp.maximum(h @ W_top2 + b_top2, 0.0)
    y = h @ W_top3
    return y

_drawn_inputs = setup_inputs


def setup_inputs(seed=0):
    import zlib

    import numpy as np

    out = dict(_drawn_inputs(seed))
    spreads = {'b_top1': (0.0, 0.1),
     'b_top2': (0.0, 0.1),
     'L0_rec_b1': (0.0, 0.1),
     'L0_rec_b2': (0.0, 0.1)}
    factors = {'tbl_0': 4.375,
     'tbl_1': 4.583,
     'tbl_2': 7.741,
     'tbl_3': 6.395,
     'tbl_4': 6.939,
     'tbl_5': 7.185,
     'tbl_6': 6.181,
     'tbl_7': 4.755,
     'tbl_8': 8.0,
     'tbl_9': 8.0,
     'tbl_10': 6.577,
     'tbl_11': 6.109,
     'tbl_12': 5.287,
     'tbl_14': 8.0,
     'tbl_15': 6.438,
     'tbl_16': 7.571,
     'tbl_17': 4.786,
     'tbl_18': 5.919,
     'tbl_19': 4.647,
     'tbl_20': 8.0,
     'tbl_21': 3.396,
     'tbl_22': 8.0,
     'tbl_23': 7.61,
     'tbl_24': 7.928,
     'tbl_25': 5.193,
     'tbl_26': 4.68,
     'tbl_27': 6.379,
     'tbl_28': 8.0,
     'tbl_29': 5.429,
     'tbl_30': 5.328,
     'tbl_31': 3.244,
     'tbl_32': 8.0,
     'tbl_33': 7.509,
     'tbl_34': 7.621,
     'tbl_35': 7.676,
     'tbl_36': 8.0,
     'tbl_37': 8.0,
     'tbl_38': 6.373,
     'tbl_13': 4.156}
    for name, (base, spread) in spreads.items():
        noise = np.random.default_rng([zlib.crc32(name.encode()), seed]).standard_normal(out[name].shape)
        drawn = base * np.exp(spread * noise) if base else spread * noise
        out[name] = jnp.asarray(drawn.astype(out[name].dtype))
    for name, factor in factors.items():
        out[name] = (out[name] * factor).astype(out[name].dtype)
    return out
```

```python
import concourse.bass as bass
from concourse import mybir
from contextlib import ExitStack

TABLES = 39


def build_tower(nc, dense_t, ids, tables, w1_fwd, w1_rev, b1, w2_t, b2, w_top1, b_top1, w_top2,
                b_top2, w_top3, y_out):
    F32, F32R, I32 = mybir.dt.float32, mybir.dt.float32r, mybir.dt.int32
    ALU = mybir.AluOpType
    ACT = mybir.ActivationFunctionType
    AX = mybir.AxisListType.X
    P = 128

    BATCH, FIELDS = ids.shape
    D = tables[0].shape[1]
    S = b1.shape[0]
    BLOCKS = BATCH // P
    TILES = 4
    STEPS_PER_BLOCK = D // TILES
    STEPS = BLOCKS * STEPS_PER_BLOCK
    SHIFTS = (FIELDS + 1) // 2
    PAIRS = FIELDS * SHIFTS
    KT = -(-PAIRS // P)
    KR = 112
    k_rows = [min(KR, PAIRS - KR * t) for t in range(KT)]
    WIDE = FIELDS + SHIFTS - 1
    STEP_X0 = WIDE * TILES
    FD = FIELDS * TILES
    NS = TILES * P

    GM = 4
    groups = [(g, min(GM, FIELDS - GM * g)) for g in range(-(-FIELDS // GM))]
    NG = len(groups)
    V_GROUPS, A_GROUPS = groups[0::2], groups[1::2]
    NV, NA = len(V_GROUPS), len(A_GROUPS)
    V_OPS = sum(n for _, n in V_GROUPS)
    ADDS = NA - 1
    V_RING, A_RING = 2, 4
    PROD_RING = 4
    assert (TILES * NV) % V_RING == 0 and (TILES * NA) % A_RING == 0 and (TILES * NA) % PROD_RING == 0

    Z_CHUNKS = 5
    ZS = SHIFTS // Z_CHUNKS
    GATHER_STEPS = 3
    HID1, HID2 = w_top1.shape[1], w_top2.shape[1]
    C1, C2 = HID1 // P, HID2 // P
    DENSE = dense_t.shape[0]

    ctx = ExitStack()
    with ctx:
        def sb(name, shape, dt=F32):
            return ctx.enter_context(nc.sbuf_tensor(name, shape, dt))

        def pb(name, shape):
            return ctx.enter_context(nc.psum_tensor(name, shape, F32))

        def sem(name):
            return ctx.enter_context(nc.semaphore(name))

        ids_sb = sb("ids_sb", [P, BLOCKS * FIELDS], I32)
        ids_blk = sb("ids_blk", [P, FIELDS], I32)
        rows = sb("rows", [P, FIELDS * D])
        x0 = sb("x0", [P, STEPS * STEP_X0])
        pairs = sb("pairs", [P, PAIRS * TILES])
        pairs_t = sb("pairs_t", [KR, KT, NS])
        ident = sb("ident", [P, P])
        ones = sb("ones", [P, P])
        w1f = sb("w1f", [KR, KT, S])
        w1r = sb("w1r", [KR, KT, S])
        w1s = sb("w1s", [KR, KT, S])
        w2 = sb("w2", [S, FIELDS * S])
        w2_hi = sb("w2_hi", [S, FIELDS * S], F32R)
        w2_lo = sb("w2_lo", [S, FIELDS * S], F32R)
        b1c = sb("b1c", [S, 1])
        b2r = sb("b2r", [P, S])
        x1 = sb("x1", [S, NS])
        x1_hi = sb("x1_hi", [S, NS], F32R)
        x1_lo = sb("x1_lo", [S, NS], F32R)
        prod = sb("prod", [P, PROD_RING, GM * S])
        psum_g = sb("psum_g", [P, 2, GM * S])
        acc = sb("acc", [P, 2, 2 * S])
        fold = sb("fold", [P, 2 * S])
        total = sb("total", [P, S])
        p1 = sb("p1", [S, STEPS * P])
        p2 = sb("p2", [P, STEPS * S])
        p1_t = sb("p1_t", [S, BATCH])
        p2_n = sb("p2_n", [P, BLOCKS, S])
        p2_t = sb("p2_t", [S, BATCH])
        dense = sb("dense", [DENSE, BATCH])
        wt1 = sb("wt1", [P, 2, HID1])
        wt1_dense = sb("wt1_dense", [DENSE, HID1])
        wt2 = sb("wt2", [P, C1, HID2])
        wt3 = sb("wt3", [P, C2])
        bt1 = sb("bt1", [P, C1])
        bt2 = sb("bt2", [P, C2])
        hid1 = sb("hid1", [P, C1, BATCH])
        hid2 = sb("hid2", [P, C2, BATCH])
        y_sb = sb("y_sb", [1, BATCH])

        yv = [pb(f"yv{i}", [P, GM * S]) for i in range(V_RING)]
        ya = [pb(f"ya{i}", [P, GM * S]) for i in range(A_RING)]
        pt = pb("pt", [P, NS])
        x1_ps = pb("x1_ps", [P, NS])

        ids_in = sem("ids_in")
        w1_in = sem("w1_in")
        w2_in = sem("w2_in")
        bias_in = sem("bias_in")
        mlp_in = sem("mlp_in")
        ones_set = sem("ones_set")
        ident_set = sem("ident_set")
        ids_staged = sem("ids_staged")
        rows_in = sem("rows_in")
        x0_ready = sem("x0_ready")
        w1_fold = sem("w1_fold")
        w2_hi_set = sem("w2_hi_set")
        w2_lo_set = sem("w2_lo_set")
        pairs_done = sem("pairs_done")
        pt_full = sem("pt_full")
        pt_read = sem("pt_read")
        l1_done = sem("l1_done")
        x1_done = sem("x1_done")
        hi_done = sem("hi_done")
        lo_done = sem("lo_done")
        p1_done = sem("p1_done")
        ya_full = sem("ya_full")
        yv_full = sem("yv_full")
        prod_done = sem("prod_done")
        added = sem("added")
        macs = sem("macs")
        fold_a = sem("fold_a")
        fold_b = sem("fold_b")
        fold_c = sem("fold_c")
        p2_done = sem("p2_done")
        p_sums = sem("p_sums")
        p2t_full = sem("p2t_full")
        p2t_set = sem("p2t_set")
        h1_full = sem("h1_full")
        h1_set = sem("h1_set")
        h2_full = sem("h2_full")
        h2_set = sem("h2_set")
        y_full = sem("y_full")
        y_set = sem("y_set")
        y_stored = sem("y_stored")

        def x0_scalar(i, q, m):
            return x0[:, bass.ds(i * STEP_X0 + (m * TILES + q), 1)]

        def w2_cols(w, g, n):
            return w[:, GM * g * S:(GM * g + n) * S]

        block = ctx.enter_context(nc.Block())

        @block.sync
        def _(sp):
            sp.dma_start(ids_sb[:].rearrange("p (k f) -> p k f", f=FIELDS),
                         ids.rearrange("(k p) f -> p k f", p=P)).then_inc(ids_in, 16)
            sp.dma_start(w2[:], w2_t).then_inc(w2_in, 16)
            full = KR * (KT - 1)
            for dst, src in ((w1f, w1_fwd), (w1r, w1_rev)):
                sp.dma_start(dst[:, 0:KT - 1, :],
                             src[0:full, :].rearrange("(t p) s -> p t s", p=KR)).then_inc(w1_in, 16)
                sp.dma_start(dst[0:k_rows[-1], KT - 1, :], src[full:PAIRS, :]).then_inc(w1_in, 16)
            sp.dma_start(b1c[:], b1.rearrange("(s a) -> s a", a=1)).then_inc(bias_in, 16)
            sp.dma_start(b2r[:], b2.partition_broadcast(P)).then_inc(bias_in, 16)
            sp.dma_start(dense[:], dense_t).then_inc(mlp_in, 16)
            sp.dma_start(wt1[:], w_top1[0:2 * P, :].rearrange("(k p) n -> p k n", p=P)).then_inc(mlp_in, 16)
            sp.dma_start(wt1_dense[:], w_top1[2 * P:2 * P + DENSE, :]).then_inc(mlp_in, 16)
            sp.dma_start(wt2[:], w_top2.rearrange("(k p) n -> p k n", p=P)).then_inc(mlp_in, 16)
            sp.dma_start(wt3[:], w_top3).then_inc(mlp_in, 16)
            sp.dma_start(bt1[:], b_top1).then_inc(mlp_in, 16)
            sp.dma_start(bt2[:], b_top2).then_inc(mlp_in, 16)
            sp.wait_ge(y_set, 1)
            sp.dma_start(y_out.rearrange("b a -> a b"), y_sb[:]).then_inc(y_stored, 16)
            sp.wait_ge(y_stored, 16)

        @block.gpsimd
        def _(pool):
            def stage_ids(blk):
                nc.gpsimd.tensor_copy(ids_blk[:], ids_sb[:, bass.ds(blk * FIELDS, FIELDS)]).then_inc(ids_staged, 1)
                pool.wait_ge(ids_staged, blk + 1)

            def gather(fields):
                for f in fields:
                    nc.gpsimd.indirect_dma_start(
                        out=rows[:, f * D:(f + 1) * D], out_offset=None, in_=tables[f],
                        in_offset=bass.IndirectOffsetOnAxis(ap=ids_blk[:, f:f + 1], axis=0)).then_inc(rows_in, 16)

            def spread_x0(blk):
                pool.wait_ge(rows_in, (blk + 1) * (16 * FIELDS))
                src = rows[:].rearrange("p (f k t) -> p k f t", k=STEPS_PER_BLOCK, t=TILES)
                n = STEPS_PER_BLOCK * STEP_X0
                dst = x0[:, bass.ds(blk * n, n)].rearrange("p (k f t) -> p k f t", k=STEPS_PER_BLOCK, t=TILES)
                for k in range(STEPS_PER_BLOCK):
                    nc.gpsimd.tensor_copy(dst[:, k, 0:FIELDS], src[:, k])
                    last = nc.gpsimd.tensor_copy(dst[:, k, FIELDS:WIDE], src[:, k, 0:WIDE - FIELDS])
                last.then_inc(x0_ready, STEPS_PER_BLOCK)

            def add_tile(i, q):
                tile = i * TILES + q
                for j in range(ADDS):
                    n = A_GROUPS[j + 1][1] * S
                    slot = (q * NA + j + 1) % PROD_RING
                    out = psum_g[:, q % 2, 0:n]
                    pool.wait_ge(prod_done, tile * NA + (j + 2))
                    if j == 0:
                        if not (isinstance(i, int) and i == 0 and q < 2):
                            pool.wait_ge(fold_a, tile - 1)
                        before = prod[:, (q * NA) % PROD_RING, 0:n]
                    else:
                        pool.wait_ge(added, tile * ADDS + j)
                        before = out
                    nc.gpsimd.tensor_tensor(out, before, prod[:, slot, 0:n], ALU.add).then_inc(added, 1)

            def block_of_steps(blk, gathers):
                per_tile = -(-FIELDS // (GATHER_STEPS * TILES))
                if gathers:
                    pool.wait_ge(x0_ready, (blk + 1) * STEPS_PER_BLOCK)
                    stage_ids(blk + 1)
                for k in range(STEPS_PER_BLOCK):
                    for q in range(TILES):
                        add_tile(blk * STEPS_PER_BLOCK + k, q)
                        if gathers and k < GATHER_STEPS:
                            f = (k * TILES + q) * per_tile
                            gather(range(min(f, FIELDS), min(f + per_tile, FIELDS)))
                    if gathers and k == GATHER_STEPS - 1:
                        spread_x0(blk + 1)

            pool.wait_ge(ids_in, 16)
            stage_ids(0)
            gather(range(FIELDS))
            nc.gpsimd.memset(ones[:], 1.0).then_inc(ones_set, 1)
            pool.wait_ge(ones_set, 1)
            nc.gpsimd.affine_select(out=ident[:], in_=ones[:], compare_op=ALU.is_equal, fill=0.0, base=0,
                                    pattern=[[-1, P]], channel_multiplier=1).then_inc(ident_set, 1)
            spread_x0(0)
            block_of_steps(0, True)
            with nc.gpsimd.Fori(1, BLOCKS - 1) as blk:
                block_of_steps(blk, True)
            block_of_steps(BLOCKS - 1, False)

        def pt_at(t):
            return 2 * t + 1

        def l1_at(t):
            return 2 * t + 4

        def next_step_work(q, g):
            pos = (q - 1) * NG + g
            if q in (1, 2):
                return [("pt", t) for t in range(KT) if pt_at(t) == pos] + \
                       [("l1", t) for t in range(KT) if l1_at(t) == pos]
            return []

        @block.tensor
        def _(pe):
            def transpose_pairs(i, t):
                pe.wait_ge(pairs_done, (i + 1) * Z_CHUNKS)
                if not (isinstance(i, int) and i == 0 and t == 0):
                    pe.wait_ge(pt_read, i * KT + t)
                n = k_rows[t]
                src = pairs[:].rearrange("p (k t) -> p t k", t=TILES)
                for q in range(TILES):
                    last = nc.tensor.transpose(pt[0:n, q * P:(q + 1) * P], src[:, q, KR * t:KR * t + n], ident[:])
                last.then_inc(pt_full, 1)

            def layer1(i, t):
                pe.wait_ge(pt_read, i * KT + (t + 1))
                if t == 0 and not (isinstance(i, int) and i == 0):
                    pe.wait_ge(x1_done, i)
                n = k_rows[t]
                last = nc.tensor.matmul(x1_ps[:], w1s[0:n, t, :], pairs_t[0:n, t, :],
                                        start=(t == 0), stop=(t == KT - 1))
                if t == KT - 1:
                    last.then_inc(l1_done, 1)

            def layer2(i, q, g, n):
                tile = i * TILES + q
                k = g // 2
                static = isinstance(i, int)
                if g % 2 == 0:
                    if not (static and tile * NV + k < V_RING):
                        back = k - V_RING
                        done = sum(m for _, m in V_GROUPS[:back % NV + 1]) + (back // NV) * V_OPS
                        pe.wait_ge(macs, tile * V_OPS + done)
                    bank, full = yv[(q * NV + k) % V_RING], yv_full
                else:
                    if not (static and tile * NA + k < A_RING):
                        pe.wait_ge(prod_done, tile * NA + (k - A_RING + 1))
                    bank, full = ya[(q * NA + k) % A_RING], ya_full
                out = bank[:, 0:n * S]
                hi, lo = x1_hi[:, q * P:(q + 1) * P], x1_lo[:, q * P:(q + 1) * P]
                nc.tensor.matmul(out, hi, w2_cols(w2_hi, g, n), start=True, stop=False)
                nc.tensor.matmul(out, hi, w2_cols(w2_lo, g, n), start=False, stop=False)
                nc.tensor.matmul(out, lo, w2_cols(w2_hi, g, n), start=False, stop=True).then_inc(full, 1)

            def step(i, last):
                for q in range(TILES):
                    if q == 0:
                        pe.wait_ge(lo_done, i * 2 + 1)
                    if q == TILES - 1:
                        pe.wait_ge(lo_done, i * 2 + 2)
                    for g, n in groups:
                        layer2(i, q, g, n)
                        for kind, t in ([] if last else next_step_work(q, g)):
                            (transpose_pairs if kind == "pt" else layer1)(i + 1, t)

            pe.wait_ge(ident_set, 1)
            for t in range(KT):
                transpose_pairs(0, t)
                if t == 0:
                    pe.wait_ge(w1_fold, 2)
                if t > 0:
                    layer1(0, t - 1)
            layer1(0, KT - 1)
            pe.wait_ge(w2_hi_set, 1)
            pe.wait_ge(w2_lo_set, 1)
            step(0, False)
            with nc.tensor.Fori(1, STEPS - 1) as i:
                step(i, False)
            step(STEPS - 1, True)

            pe.wait_ge(mlp_in, 16 * 7)
            pe.wait_ge(p_sums, 2)
            for k in range(BLOCKS):
                last = nc.tensor.transpose(pt[:, k * P:(k + 1) * P], p2_n[:, k, :], ident[:])
            last.then_inc(p2t_full, 1)
            for c in range(C1):
                cols = slice(c * P, (c + 1) * P)
                nc.tensor.matmul(ya[c][:], wt1[:, 0, cols], p1_t[:], start=True, stop=False)
                nc.tensor.matmul(ya[c][:], wt1_dense[:, cols], dense[:], start=False, stop=False)
                pe.wait_ge(p2t_set, 1)
                nc.tensor.matmul(ya[c][:], wt1[:, 1, cols], p2_t[:], start=False, stop=True).then_inc(h1_full, 1)
            for k in range(C1):
                pe.wait_ge(h1_set, k + 1)
                for c in range(C2):
                    last = nc.tensor.matmul(yv[c][:], wt2[:, k, c * P:(c + 1) * P], hid1[:, k, :],
                                            start=(k == 0), stop=(k == C1 - 1))
                    if k == C1 - 1:
                        last.then_inc(h2_full, 1)
            for k in range(C2):
                pe.wait_ge(h2_set, k + 1)
                last = nc.tensor.matmul(x1_ps[0:1, :], wt3[:, k:k + 1], hid2[:, k, :],
                                        start=(k == 0), stop=(k == C2 - 1))
            last.then_inc(y_full, 1)

        @block.scalar
        def _(act):
            def copy_pairs(i, t):
                act.wait_ge(pt_full, i * KT + (t + 1))
                if t == 0 and not (isinstance(i, int) and i == 0):
                    act.wait_ge(l1_done, i)
                n = k_rows[t]
                nc.scalar.copy(pairs_t[0:n, t, :], pt[0:n, :]).then_inc(pt_read, 1)

            def relu_x1(i):
                act.wait_ge(l1_done, i + 1)
                if not (isinstance(i, int) and i == 0):
                    act.wait_ge(lo_done, i * 2)
                    act.wait_ge(p1_done, i)
                nc.scalar.activation(x1[:], x1_ps[:], ACT.Relu, bias=b1c[:, 0:1]).then_inc(x1_done, 1)

            def split_hi(i, part):
                cols = slice(0, NS - P) if part == 0 else slice(NS - P, NS)
                act.wait_ge(x1_done, i + 1)
                if not (isinstance(i, int) and i == 0):
                    act.wait_ge(ya_full, i * (TILES * NA) - (NA if part == 0 else 0))
                nc.scalar.copy(x1_hi[:, cols], x1[:, cols]).then_inc(hi_done, 1)

            def products(i, q, k):
                g, n = A_GROUPS[k]
                tile = i * TILES + q
                act.wait_ge(ya_full, tile * NA + (k + 1))
                if not (isinstance(i, int) and tile * NA + k < PROD_RING):
                    back = k - PROD_RING
                    act.wait_ge(added, tile * ADDS + ((back // NA) * ADDS + max(back % NA, 1)))
                bank = ya[(q * NA + k) % A_RING]
                slot = (q * NA + k) % PROD_RING
                for j in range(n):
                    last = nc.scalar.activation(prod[:, slot, j * S:(j + 1) * S], bank[:, j * S:(j + 1) * S],
                                                ACT.Copy, scale=x0_scalar(i, q, GM * g + j))
                last.then_inc(prod_done, 1)

            def step(i, last):
                act.wait_ge(x0_ready, i + 1)
                for q in range(TILES):
                    for g, _n in groups:
                        if g % 2:
                            products(i, q, g // 2)
                        if not last:
                            for kind, t in next_step_work(q, g):
                                if kind == "pt":
                                    copy_pairs(i + 1, t)
                            if (q, g) == (2, 7):
                                relu_x1(i + 1)
                            if (q, g) == (3, 1):
                                split_hi(i + 1, 0)
                            if (q, g) == (3, NG - 1):
                                split_hi(i + 1, 1)

            act.wait_ge(w2_in, 16)
            nc.scalar.copy(w2_hi[:], w2[:]).then_inc(w2_hi_set, 1)
            act.wait_ge(bias_in, 32)
            for t in range(KT):
                copy_pairs(0, t)
            relu_x1(0)
            split_hi(0, 0)
            split_hi(0, 1)
            step(0, False)
            with nc.scalar.Fori(1, STEPS - 1) as i:
                step(i, False)
            step(STEPS - 1, True)

            act.wait_ge(p2t_full, 1)
            nc.scalar.copy(p2_t[:], pt[:]).then_inc(p2t_set, 1)
            act.wait_ge(mlp_in, 16 * 7)
            for c in range(C1):
                act.wait_ge(h1_full, c + 1)
                nc.scalar.activation(hid1[:, c, :], ya[c][:], ACT.Relu, bias=bt1[:, c:c + 1]).then_inc(h1_set, 1)
            for c in range(C2):
                act.wait_ge(h2_full, c + 1)
                nc.scalar.activation(hid2[:, c, :], yv[c][:], ACT.Relu, bias=bt2[:, c:c + 1]).then_inc(h2_set, 1)
            act.wait_ge(y_full, 1)
            nc.scalar.copy(y_sb[:], x1_ps[0:1, :]).then_inc(y_set, 1)

        @block.vector
        def _(dve):
            def multiply_pairs(i, c):
                if c == 0:
                    dve.wait_ge(x0_ready, i + 1)
                    if not (isinstance(i, int) and i == 0):
                        dve.wait_ge(pt_full, i * KT)
                near = x0[:, bass.ds(i * STEP_X0, FD)]
                far = x0[:, bass.ds(i * STEP_X0 + c * ZS * TILES, FD)]
                part = list(near.ap[0])
                near = bass.AP(near.tensor, near.offset, [part, [0, ZS], [1, FD]])
                far = bass.AP(far.tensor, far.offset, [part, [TILES, ZS], [1, FD]])
                out = pairs[:, c * ZS * FD:(c + 1) * ZS * FD].rearrange("p (z f) -> p z f", z=ZS)
                nc.vector.tensor_tensor(out, near, far, ALU.mult).then_inc(pairs_done, 1)

            def split_lo(i, part):
                cols = slice(0, NS - P) if part == 0 else slice(NS - P, NS)
                dve.wait_ge(hi_done, i * 2 + (part + 1))
                nc.vector.tensor_tensor(x1_lo[:, cols], x1[:, cols], x1_hi[:, cols], ALU.subtract).then_inc(lo_done, 1)

            def sum_x1(i):
                dve.wait_ge(x1_done, i + 1)
                nc.vector.tensor_reduce(p1[:, bass.ds(i * P, P)], x1[:].rearrange("s (q b) -> s b q", b=P),
                                        AX, ALU.add).then_inc(p1_done, 1)

            def mac_group(i, q, k):
                g, n = V_GROUPS[k]
                tile = i * TILES + q
                dve.wait_ge(yv_full, tile * NV + (k + 1))
                bank = yv[(q * NV + k) % V_RING]
                for j in range(n):
                    op = GM * k + j
                    half = acc[:, q % 2, (op % 2) * S:(op % 2 + 1) * S]
                    y = bank[:, j * S:(j + 1) * S]
                    x = x0_scalar(i, q, GM * g + j)
                    if op == 0:
                        nc.vector.scalar_tensor_tensor(out=half, in0=y, scalar=x, in1=b2r[:], op0=ALU.mult,
                                                       op1=ALU.add).then_inc(macs, 1)
                    elif op == 1:
                        nc.vector.tensor_scalar(half, y, x, None, ALU.mult).then_inc(macs, 1)
                    else:
                        dve.wait_ge(macs, tile * V_OPS + (op - 1))
                        nc.vector.scalar_tensor_tensor(out=half, in0=y, scalar=x, in1=half, op0=ALU.mult,
                                                       op1=ALU.add).then_inc(macs, 1)

            def finish_tile(i, q, part):
                tile = i * TILES + q
                if part == 0:
                    dve.wait_ge(added, (tile + 1) * ADDS)
                    if not (isinstance(i, int) and tile == 0):
                        dve.wait_ge(fold_c, tile)
                    g = psum_g[:, q % 2, :]
                    nc.vector.tensor_tensor(fold[:], g[:, 0:2 * S], g[:, 2 * S:4 * S], ALU.add).then_inc(fold_a, 1)
                if part == 1:
                    dve.wait_ge(fold_a, tile + 1)
                    dve.wait_ge(macs, (tile + 1) * V_OPS)
                    nc.vector.tensor_tensor(fold[:], fold[:], acc[:, q % 2, :], ALU.add).then_inc(fold_b, 1)
                if part == 2:
                    dve.wait_ge(fold_b, tile + 1)
                    if not (isinstance(i, int) and tile == 0):
                        dve.wait_ge(p2_done, tile)
                    nc.vector.tensor_tensor(total[:], fold[:, 0:S], fold[:, S:2 * S], ALU.add).then_inc(fold_c, 1)
                if part == 3:
                    dve.wait_ge(fold_c, tile + 1)
                    out = p2[:, bass.ds(i * S, S)]
                    if q == 0:
                        nc.vector.tensor_scalar(out, total[:], 0.0, None, ALU.max).then_inc(p2_done, 1)
                    else:
                        dve.wait_ge(p2_done, tile)
                        nc.vector.scalar_tensor_tensor(out=out, in0=total[:], scalar=0.0, in1=out, op0=ALU.max,
                                                       op1=ALU.add).then_inc(p2_done, 1)

            def step(i, first, last):
                for q in range(TILES):
                    for k in range(NV):
                        mac_group(i, q, k)
                        if k >= 1:
                            if q > 0:
                                finish_tile(i, q - 1, k - 1)
                            elif not first:
                                finish_tile(i - 1, TILES - 1, k - 1)
                        if q == 0 and not last:
                            multiply_pairs(i + 1, k)
                        if (q, k) == (1, 0):
                            sum_x1(i)
                        if (q, k) == (3, 1) and not last:
                            split_lo(i + 1, 0)
                if not last:
                    split_lo(i + 1, 1)

            dve.wait_ge(w1_in, 16 * 4)
            nc.vector.tensor_tensor(w1s[:, 0:KT - 1, :], w1f[:, 0:KT - 1, :], w1r[:, 0:KT - 1, :],
                                    ALU.add).then_inc(w1_fold, 1)
            dve.wait_ge(w1_fold, 1)
            nc.vector.tensor_copy(w1s[0:FIELDS, 0, :], w1f[0:FIELDS, 0, :])
            nc.vector.tensor_tensor(w1s[0:k_rows[-1], KT - 1, :], w1f[0:k_rows[-1], KT - 1, :],
                                    w1r[0:k_rows[-1], KT - 1, :], ALU.add).then_inc(w1_fold, 1)
            dve.wait_ge(w2_hi_set, 1)
            nc.vector.tensor_tensor(w2_lo[:], w2[:], w2_hi[:], ALU.subtract).then_inc(w2_lo_set, 1)
            dve.wait_ge(bias_in, 32)
            for c in range(Z_CHUNKS):
                multiply_pairs(0, c)
            split_lo(0, 0)
            split_lo(0, 1)
            step(0, True, False)
            with nc.vector.Fori(1, STEPS - 1) as i:
                step(i, False, False)
            step(STEPS - 1, False, True)
            for part in range(4):
                finish_tile(STEPS - 1, TILES - 1, part)
            dve.wait_ge(p1_done, STEPS)
            nc.vector.tensor_reduce(p1_t[:].rearrange("s (k b) -> s k b", b=P),
                                    p1[:].rearrange("s (k j b) -> s k b j", k=BLOCKS, b=P),
                                    AX, ALU.add).then_inc(p_sums, 1)
            dve.wait_ge(p2_done, STEPS * TILES)
            nc.vector.tensor_reduce(p2_n[:], p2[:].rearrange("p (k j s) -> p k s j", k=BLOCKS, s=S),
                                    AX, ALU.add).then_inc(p_sums, 1)


def kernel(**inputs):
    import numpy as np
    import concourse.bacc as bacc
    from concourse import mybir as mb
    from concourse.bass_utils import run_bass_kernel_spmd

    fields = TABLES
    shifts = (fields + 1) // 2
    m = np.tile(np.arange(fields), shifts)
    far = (m + np.repeat(np.arange(shifts), fields)) % fields
    w1 = np.asarray(inputs["L0_rec_W1"])

    def columns(a):
        return np.asarray(a).reshape(-1, 128).T

    arrays = {
        "dense_t": np.asarray(inputs["dense_ctx"]).T,
        "ids": inputs["ids"],
        **{f"tbl_{f}": inputs[f"tbl_{f}"] for f in range(fields)},
        "w1_fwd": w1[:, m, far].T,
        "w1_rev": w1[:, far, m].T,
        "b1": inputs["L0_rec_b1"],
        "w2_t": np.asarray(inputs["L0_rec_W2"]).transpose(1, 2, 0).reshape(128, -1),
        "b2": inputs["L0_rec_b2"],
        "w_top1": inputs["W_top1"], "b_top1": columns(inputs["b_top1"]),
        "w_top2": inputs["W_top2"], "b_top2": columns(inputs["b_top2"]),
        "w_top3": columns(inputs["W_top3"]),
    }
    arrays = {k: np.ascontiguousarray(a) for k, a in arrays.items()}
    batch = arrays["ids"].shape[0]
    nc = bacc.Bacc("TRN2", target_bir_lowering=False, num_devices=1)
    aps = {k: nc.dram_tensor(k, a.shape, mb.dt.from_np(a.dtype), kind="ExternalInput").ap() for k, a in arrays.items()}
    tables = [aps.pop(f"tbl_{f}") for f in range(fields)]
    y_out = nc.dram_tensor("y_out", (batch, 1), mb.dt.float32, kind="ExternalOutput").ap()
    build_tower(nc, tables=tables, y_out=y_out, **aps)
    result = run_bass_kernel_spmd(nc, [arrays], core_ids=[0])
    return result.results[0]["y_out"]
```

```python
import concourse.bass as bass
from concourse import mybir
from contextlib import ExitStack

TABLES = 39


def build_tower(nc, dense_t, ids, tables, w1_fwd, w1_rev, b1, w2_t, b2, w_top1, b_top1, w_top2,
                b_top2, w_top3, y_out):
    F32, F32R, I32 = mybir.dt.float32, mybir.dt.float32r, mybir.dt.int32
    ALU = mybir.AluOpType
    ACT = mybir.ActivationFunctionType
    AX = mybir.AxisListType.X
    P = 128

    BATCH, FIELDS = ids.shape
    D = tables[0].shape[1]
    S = b1.shape[0]
    BLOCKS = BATCH // P
    TILES = 4
    STEPS_PER_BLOCK = D // TILES
    STEPS = BLOCKS * STEPS_PER_BLOCK
    LEAD = 2
    SHIFTS = (FIELDS + 1) // 2
    PAIRS = FIELDS * SHIFTS
    KS = P // FIELDS
    KR = KS * FIELDS
    KT = -(-SHIFTS // KS)
    k_rows = [min(KR, PAIRS - KR * t) for t in range(KT)]
    WIDE = FIELDS + SHIFTS - 1
    STEP_X0 = FIELDS * TILES
    NS = TILES * P
    PAIR = 2

    GM = 4
    KINDS = "AVAVAAVAAV"
    NG = len(KINDS)
    groups = [(g, min(GM, FIELDS - GM * g)) for g in range(NG)]
    V_GROUPS = [x for x in groups if KINDS[x[0]] == "V"]
    A_GROUPS = [x for x in groups if KINDS[x[0]] == "A"]
    NV, NA = len(V_GROUPS), len(A_GROUPS)
    V_OPS = sum(n for _, n in V_GROUPS)
    ADDS = NA - 2
    V_RING, A_RING = 2, 4
    assert (TILES * NV) % V_RING == 0 and (TILES * NA) % A_RING == 0
    assert KINDS[-1] == "V" and GM * NG >= FIELDS and all(n == GM for _, n in A_GROUPS)

    T_AT = 20
    STAGE_AT = T_AT - 3
    X0T_AT = T_AT + 2
    L1_AT = [11, 14, 18, 21, 25, 28, 32]
    PAIRS_AT = [at - 4 for at in L1_AT]
    RELU_AT = L1_AT[-1] + 1
    LO_AT = RELU_AT + 2
    P1_AT = 3
    FAR0_BY = "VAVVAAA"
    FINISH_AT = [(2, 1), (2, 2), (2, 3), (3, 0), (3, 1)]

    HID1, HID2 = w_top1.shape[1], w_top2.shape[1]
    C1, C2 = HID1 // P, HID2 // P
    DENSE = dense_t.shape[0]

    ctx = ExitStack()
    with ctx:
        def sb(name, shape, dt=F32):
            return ctx.enter_context(nc.sbuf_tensor(name, shape, dt))

        def pb(name, shape):
            return ctx.enter_context(nc.psum_tensor(name, shape, F32))

        def sem(name):
            return ctx.enter_context(nc.semaphore(name))

        ids_sb = sb("ids_sb", [P, BLOCKS * FIELDS], I32)
        ids_blk = sb("ids_blk", [P, FIELDS], I32)
        rows = sb("rows", [P, WIDE * D])
        x0 = sb("x0", [P, STEPS * STEP_X0])
        factors0 = sb("factors0", [P, KT + 1, TILES * KR])
        x0_step = sb("x0_step", [P, STEP_X0])
        x0_t = sb("x0_t", [PAIR * FIELDS, TILES // PAIR, P])
        scratch = nc.dram_tensor("x0_scratch", (WIDE, NS), F32, kind="Internal").ap()
        near = sb("near", [KR, NS])
        far = sb("far", [KR, KT, NS])
        pairs = sb("pairs", [KR, KT, NS])
        ident = sb("ident", [P, P])
        ones = sb("ones", [P, P])
        w1f = sb("w1f", [KR, KT, S])
        w1r = sb("w1r", [KR, KT, S])
        w1s = sb("w1s", [KR, KT, S])
        w2 = sb("w2", [S, FIELDS * S])
        w2_hi = sb("w2_hi", [S, FIELDS * S], F32R)
        w2_lo = sb("w2_lo", [S, FIELDS * S], F32R)
        b1c = sb("b1c", [S, 1])
        b2r = sb("b2r", [P, S])
        x1 = sb("x1", [S, NS])
        x1_hi = sb("x1_hi", [S, NS], F32R)
        x1_lo = sb("x1_lo", [S, NS], F32R)
        prod = sb("prod", [P, NA, GM * S])
        psum_g = sb("psum_g", [P, 2, GM * S])
        acc = sb("acc", [P, 2, 2 * S])
        fold = sb("fold", [P, GM * S])
        total = sb("total", [P, S])
        p1 = sb("p1", [S, STEPS * P])
        p2 = sb("p2", [P, STEPS * S])
        p1_t = sb("p1_t", [S, BATCH])
        p2_n = sb("p2_n", [P, BLOCKS, S])
        p2_t = sb("p2_t", [S, BATCH])
        dense = sb("dense", [DENSE, BATCH])
        wt1 = sb("wt1", [P, 2, HID1])
        wt1_dense = sb("wt1_dense", [DENSE, HID1])
        wt2 = sb("wt2", [P, C1, HID2])
        wt3 = sb("wt3", [P, C2])
        bt1 = sb("bt1", [P, C1])
        bt2 = sb("bt2", [P, C2])
        hid1 = sb("hid1", [P, C1, BATCH])
        hid2 = sb("hid2", [P, C2, BATCH])
        y_sb = sb("y_sb", [1, BATCH])

        yv = [pb(f"yv{i}", [P, GM * S]) for i in range(V_RING)]
        ya = [pb(f"ya{i}", [P, GM * S]) for i in range(A_RING)]
        x0_ps = pb("x0_ps", [PAIR * FIELDS, TILES // PAIR * P])
        x1_ps = pb("x1_ps", [P, NS])
        far0_banks = yv + ya

        ids_in = sem("ids_in")
        w1_in = sem("w1_in")
        w2_in = sem("w2_in")
        bias_in = sem("bias_in")
        mlp_in = sem("mlp_in")
        ones_set = sem("ones_set")
        ident_set = sem("ident_set")
        ids_staged = sem("ids_staged")
        rows_in = sem("rows_in")
        x0_ready = sem("x0_ready")
        w1_fold = sem("w1_fold")
        w2_hi_set = sem("w2_hi_set")
        w2_lo_set = sem("w2_lo_set")
        wrap_set = sem("wrap_set")
        near0_laid = sem("near0_laid")
        far0_laid_a = sem("far0_laid_a")
        far0_laid_v = sem("far0_laid_v")
        near0_full = sem("near0_full")
        near0_set = sem("near0_set")
        far0_full = sem("far0_full")
        x0_staged = sem("x0_staged")
        x0t_full = sem("x0t_full")
        x0t_set = sem("x0t_set")
        scratch_in = sem("scratch_in")
        factors_in = sem("factors_in")
        pairs_done = sem("pairs_done")
        l1_done = sem("l1_done")
        x1_done = sem("x1_done")
        hi_done = sem("hi_done")
        lo_done = sem("lo_done")
        p1_done = sem("p1_done")
        ya_full = sem("ya_full")
        yv_full = sem("yv_full")
        prod_done = sem("prod_done")
        added = sem("added")
        macs = sem("macs")
        fold_a = sem("fold_a")
        fold_b = sem("fold_b")
        fold_c = sem("fold_c")
        fold_d = sem("fold_d")
        p2_done = sem("p2_done")
        p_sums = sem("p_sums")
        p2t_full = sem("p2t_full")
        p2t_set = sem("p2t_set")
        h1_full = sem("h1_full")
        h1_set = sem("h1_set")
        h2_full = sem("h2_full")
        h2_set = sem("h2_set")
        y_full = sem("y_full")
        y_set = sem("y_set")
        y_stored = sem("y_stored")

        def factor0_rows(shift, n):
            return bass.AP(rows, (shift or 0) * D, [[WIDE * D, P], [1, TILES], [0 if shift is None else D, n],
                                                    [D, FIELDS]])

        def factor0_slot(slot, n):
            return factors0[:, slot, :].rearrange("p (q j m) -> p q j m", q=TILES, j=KS)[:, :, 0:n, :]

        def x0_scalar(i, q, m):
            return x0[:, bass.ds(i * STEP_X0 + (m * TILES + q), 1)]

        def w2_cols(w, g, n):
            return w[:, GM * g * S:(GM * g + n) * S]

        block = ctx.enter_context(nc.Block())

        @block.sync
        def _(sp):
            sp.dma_start(ids_sb[:].rearrange("p (k f) -> p k f", f=FIELDS),
                         ids.rearrange("(k p) f -> p k f", p=P)).then_inc(ids_in, 16)
            full = KR * (KT - 1)
            for dst, src in ((w1f, w1_fwd), (w1r, w1_rev)):
                sp.dma_start(dst[:, 0:KT - 1, :],
                             src[0:full, :].rearrange("(t p) s -> p t s", p=KR)).then_inc(w1_in, 16)
                sp.dma_start(dst[0:k_rows[-1], KT - 1, :], src[full:PAIRS, :]).then_inc(w1_in, 16)
            sp.dma_start(b1c[:], b1.rearrange("(s a) -> s a", a=1)).then_inc(bias_in, 16)
            sp.dma_start(b2r[:], b2.partition_broadcast(P)).then_inc(bias_in, 16)
            sp.dma_start(w2[:], w2_t).then_inc(w2_in, 16)
            sp.dma_start(dense[:], dense_t).then_inc(mlp_in, 16)
            sp.dma_start(wt1[:], w_top1[0:2 * P, :].rearrange("(k p) n -> p k n", p=P)).then_inc(mlp_in, 16)
            sp.dma_start(wt1_dense[:], w_top1[2 * P:2 * P + DENSE, :]).then_inc(mlp_in, 16)
            sp.dma_start(wt2[:], w_top2.rearrange("(k p) n -> p k n", p=P)).then_inc(mlp_in, 16)
            sp.dma_start(wt3[:], w_top3).then_inc(mlp_in, 16)
            sp.dma_start(bt1[:], b_top1).then_inc(mlp_in, 16)
            sp.dma_start(bt2[:], b_top2).then_inc(mlp_in, 16)

            def spread_factors(i):
                sp.wait_ge(x0t_set, i)
                for r in range(PAIR):
                    to = scratch.rearrange("f (j r b) -> f j r b", r=PAIR, b=P)[:, :, r, :]
                    of = x0_t[r * FIELDS:(r + 1) * FIELDS]
                    sp.dma_start(to[0:FIELDS], of).then_inc(scratch_in, 16)
                    sp.dma_start(to[FIELDS:WIDE], of[0:WIDE - FIELDS]).then_inc(scratch_in, 16)
                sp.wait_ge(scratch_in, i * (32 * PAIR))
                sp.wait_ge(l1_done, i)
                for j in range(KS):
                    part = slice(j * FIELDS, (j + 1) * FIELDS)
                    n = len(range(j, SHIFTS, KS))
                    src = bass.AP(scratch.tensor, j * NS, [[NS, FIELDS], [KS * NS, n], [1, NS]])
                    sp.dma_start(near[part, :], scratch[0:FIELDS, :]).then_inc(factors_in, 16)
                    sp.dma_start(far[part, 0:n, :], src).then_inc(factors_in, 16)

            with nc.sync.Fori(1, STEPS) as i:
                spread_factors(i)
            sp.wait_ge(y_set, 1)
            sp.dma_start(y_out.rearrange("b a -> a b"), y_sb[:]).then_inc(y_stored, 16)
            sp.wait_ge(y_stored, 16)

        @block.gpsimd
        def _(pool):
            def stage_ids(blk):
                nc.gpsimd.tensor_copy(ids_blk[:], ids_sb[:, bass.ds(blk * FIELDS, FIELDS)]).then_inc(ids_staged, 1)
                pool.wait_ge(ids_staged, blk + 1)

            def gather(fields):
                for f in fields:
                    nc.gpsimd.indirect_dma_start(
                        out=rows[:, f * D:(f + 1) * D], out_offset=None, in_=tables[f],
                        in_offset=bass.IndirectOffsetOnAxis(ap=ids_blk[:, f:f + 1], axis=0)).then_inc(rows_in, 16)

            def spread_x0(blk):
                pool.wait_ge(rows_in, (blk + 1) * (16 * FIELDS))
                n = STEPS_PER_BLOCK * STEP_X0
                nc.gpsimd.tensor_copy(
                    x0[:, bass.ds(blk * n, n)].rearrange("p (k f t) -> p k f t", k=STEPS_PER_BLOCK, t=TILES),
                    rows[:, 0:FIELDS * D].rearrange("p (f k t) -> p k f t", k=STEPS_PER_BLOCK, t=TILES)
                ).then_inc(x0_ready, STEPS_PER_BLOCK)

            def add_tile(i, q, fields=()):
                tile = i * TILES + q
                out = psum_g[:, q % 2, :]
                for j in range(ADDS):
                    pool.wait_ge(prod_done, tile * NA + (j + 2))
                    if j == 0:
                        if not (isinstance(i, int) and i == 0 and q < 2):
                            pool.wait_ge(fold_a, tile - 1)
                        before = prod[:, 0, :]
                    else:
                        pool.wait_ge(added, tile * ADDS + j)
                        before = out
                    nc.gpsimd.tensor_tensor(out, before, prod[:, j + 1, :], ALU.add).then_inc(added, 1)
                    gather(fields[j::ADDS])

            def steps_and_block(steps, blk, fields):
                tiles, n = len(steps) * TILES, len(fields)
                for k, i in enumerate(steps):
                    for q in range(TILES):
                        at = k * TILES + q
                        add_tile(i, q, fields[at * n // tiles:(at + 1) * n // tiles])
                spread_x0(blk)

            pool.wait_ge(ids_in, 16)
            stage_ids(0)
            gather(range(FIELDS))
            nc.gpsimd.memset(ones[:], 1.0).then_inc(ones_set, 1)
            pool.wait_ge(ones_set, 1)
            nc.gpsimd.affine_select(out=ident[:], in_=ones[:], compare_op=ALU.is_equal, fill=0.0, base=0,
                                    pattern=[[-1, P]], channel_multiplier=1).then_inc(ident_set, 1)
            spread_x0(0)
            pool.wait_ge(x0_ready, STEPS_PER_BLOCK)
            pool.wait_ge(x0_staged, 1)
            pool.wait_ge(near0_laid, 1)
            pool.wait_ge(far0_laid_a, FAR0_BY.count("A"))
            pool.wait_ge(far0_laid_v, FAR0_BY.count("V"))
            stage_ids(1)
            gather(range(FIELDS // 2))
            steps_and_block(range(STEPS_PER_BLOCK - LEAD), 1, range(FIELDS // 2, FIELDS))
            with nc.gpsimd.Fori(2, BLOCKS) as blk:
                pool.wait_ge(x0_ready, blk * STEPS_PER_BLOCK)
                stage_ids(blk)
                first = blk * STEPS_PER_BLOCK - (STEPS_PER_BLOCK + LEAD)
                steps_and_block([first + k for k in range(STEPS_PER_BLOCK)], blk, range(FIELDS))
            with nc.gpsimd.Fori(STEPS - STEPS_PER_BLOCK - LEAD, STEPS) as i:
                for q in range(TILES):
                    add_tile(i, q)

        @block.tensor
        def _(pe):
            def transpose_factor0(bank, slot, n):
                for q in range(TILES):
                    last = nc.tensor.transpose(bank[0:n, q * P:(q + 1) * P],
                                               factors0[:, slot, q * KR:q * KR + n], ident[:])
                return last

            def transpose_x0(i):
                pe.wait_ge(x0_staged, i)
                if not (isinstance(i, int) and i == 1):
                    pe.wait_ge(x0t_set, i - 1)
                n = PAIR * FIELDS
                for j in range(TILES // PAIR):
                    last = nc.tensor.transpose(x0_ps[0:n, j * P:(j + 1) * P], x0_step[:, j * n:(j + 1) * n], ident[:])
                last.then_inc(x0t_full, 1)

            def layer1(i, t):
                pe.wait_ge(pairs_done, i * KT + (t + 1))
                if t == 0 and not (isinstance(i, int) and i == 0):
                    pe.wait_ge(x1_done, i)
                n = k_rows[t]
                last = nc.tensor.matmul(x1_ps[:], w1s[0:n, t, :], pairs[0:n, t, :],
                                        start=(t == 0), stop=(t == KT - 1))
                if t == KT - 1:
                    last.then_inc(l1_done, 1)

            def layer2(i, q, g, n):
                tile = i * TILES + q
                static = isinstance(i, int)
                if KINDS[g] == "V":
                    k = V_GROUPS.index((g, n))
                    if not (static and tile * NV + k < V_RING):
                        back = k - V_RING
                        done = sum(m for _, m in V_GROUPS[:back % NV + 1]) + (back // NV) * V_OPS
                        pe.wait_ge(macs, tile * V_OPS + done)
                    bank, full = yv[(q * NV + k) % V_RING], yv_full
                else:
                    k = A_GROUPS.index((g, n))
                    if not (static and tile * NA + k < A_RING):
                        pe.wait_ge(prod_done, tile * NA + (k - A_RING + 1))
                    bank, full = ya[(q * NA + k) % A_RING], ya_full
                out = bank[:, 0:n * S]
                hi, lo = x1_hi[:, q * P:(q + 1) * P], x1_lo[:, q * P:(q + 1) * P]
                nc.tensor.matmul(out, hi, w2_cols(w2_hi, g, n), start=True, stop=False)
                nc.tensor.matmul(out, hi, w2_cols(w2_lo, g, n), start=False, stop=False)
                nc.tensor.matmul(out, lo, w2_cols(w2_hi, g, n), start=False, stop=True).then_inc(full, 1)

            def step(i, ahead):
                for q in range(TILES):
                    if q == 0:
                        pe.wait_ge(lo_done, i * 2 + 1)
                    if q == TILES - 1:
                        pe.wait_ge(lo_done, i * 2 + 2)
                    for g, n in groups:
                        layer2(i, q, g, n)
                        at = q * NG + g
                        if ahead > 1 and at == T_AT:
                            transpose_x0(i + 2)
                        if ahead > 0 and at in L1_AT:
                            layer1(i + 1, L1_AT.index(at))

            pe.wait_ge(ident_set, 1)
            pe.wait_ge(near0_laid, 1)
            transpose_factor0(x1_ps, KT, KR).then_inc(near0_full, 1)
            pe.wait_ge(w1_fold, 2)
            for t in range(KT):
                if FAR0_BY[t] == "V":
                    pe.wait_ge(far0_laid_v, FAR0_BY[:t + 1].count("V"))
                else:
                    pe.wait_ge(far0_laid_a, FAR0_BY[:t + 1].count("A"))
                if t >= len(far0_banks):
                    pe.wait_ge(pairs_done, t - len(far0_banks) + 1)
                transpose_factor0(far0_banks[t % len(far0_banks)], t, k_rows[t]).then_inc(far0_full, 1)
                if t == 2:
                    transpose_x0(1)
                if t == 3:
                    pe.wait_ge(near0_set, 1)
                if t >= 3:
                    layer1(0, t - 3)
            for t in range(KT - 3, KT):
                layer1(0, t)
            pe.wait_ge(w2_hi_set, 1)
            pe.wait_ge(w2_lo_set, 1)
            step(0, 2)
            with nc.tensor.Fori(1, STEPS - 2) as i:
                step(i, 2)
            step(STEPS - 2, 1)
            step(STEPS - 1, 0)

            pe.wait_ge(mlp_in, 16 * 7)
            pe.wait_ge(p_sums, 2)
            for k in range(BLOCKS):
                last = nc.tensor.transpose(x1_ps[:, k * P:(k + 1) * P], p2_n[:, k, :], ident[:])
            last.then_inc(p2t_full, 1)
            for c in range(C1):
                cols = slice(c * P, (c + 1) * P)
                nc.tensor.matmul(ya[c][:], wt1[:, 0, cols], p1_t[:], start=True, stop=False)
                nc.tensor.matmul(ya[c][:], wt1_dense[:, cols], dense[:], start=False, stop=False)
                pe.wait_ge(p2t_set, 1)
                nc.tensor.matmul(ya[c][:], wt1[:, 1, cols], p2_t[:], start=False, stop=True).then_inc(h1_full, 1)
            for k in range(C1):
                pe.wait_ge(h1_set, k + 1)
                for c in range(C2):
                    last = nc.tensor.matmul(yv[c][:], wt2[:, k, c * P:(c + 1) * P], hid1[:, k, :],
                                            start=(k == 0), stop=(k == C1 - 1))
                    if k == C1 - 1:
                        last.then_inc(h2_full, 1)
            for k in range(C2):
                pe.wait_ge(h2_set, k + 1)
                last = nc.tensor.matmul(x1_ps[0:1, :], wt3[:, k:k + 1], hid2[:, k, :],
                                        start=(k == 0), stop=(k == C2 - 1))
            last.then_inc(y_full, 1)

        @block.scalar
        def _(act):
            def stage_x0(i):
                if isinstance(i, int) and i == 1:
                    act.wait_ge(rows_in, 16 * FIELDS)
                    of = rows[:, 0:FIELDS * D].rearrange("p (f d) -> p f d", d=D)[:, :, TILES:2 * TILES]
                else:
                    act.wait_ge(x0_ready, i + 1)
                    act.wait_ge(x0t_full, i - 1)
                    of = x0[:, bass.ds(i * STEP_X0, STEP_X0)].rearrange("p (f t) -> p f t", t=TILES)
                nc.scalar.copy(x0_step[:].rearrange("p (t f) -> p f t", t=TILES), of).then_inc(x0_staged, 1)

            def copy_x0t(i):
                act.wait_ge(x0t_full, i)
                if not (isinstance(i, int) and i == 1):
                    act.wait_ge(scratch_in, (i - 1) * (32 * PAIR))
                    act.wait_ge(factors_in, (i - 1) * (32 * KS))
                nc.scalar.copy(x0_t[:].rearrange("p j b -> p (j b)"), x0_ps[:]).then_inc(x0t_set, 1)

            def relu_x1(i):
                act.wait_ge(l1_done, i + 1)
                if not (isinstance(i, int) and i == 0):
                    act.wait_ge(lo_done, i * 2)
                    act.wait_ge(p1_done, i)
                nc.scalar.activation(x1[:], x1_ps[:], ACT.Relu, bias=b1c[:, 0:1]).then_inc(x1_done, 1)

            def split_hi(i, part):
                cols = slice(0, NS - P) if part == 0 else slice(NS - P, NS)
                act.wait_ge(x1_done, i + 1)
                if not (isinstance(i, int) and i == 0):
                    act.wait_ge(yv_full, i * (TILES * NV) - (NV if part == 0 else 0))
                nc.scalar.copy(x1_hi[:, cols], x1[:, cols]).then_inc(hi_done, 1)

            def products(i, q, k):
                g, n = A_GROUPS[k]
                tile = i * TILES + q
                act.wait_ge(ya_full, tile * NA + (k + 1))
                if not (isinstance(i, int) and tile == 0):
                    if k <= ADDS:
                        act.wait_ge(added, (tile - 1) * ADDS + max(k, 1))
                    else:
                        act.wait_ge(fold_a, tile)
                bank = ya[(q * NA + k) % A_RING]
                for j in range(n):
                    last = nc.scalar.activation(prod[:, k, j * S:(j + 1) * S], bank[:, j * S:(j + 1) * S],
                                                ACT.Copy, scale=x0_scalar(i, q, GM * g + j))
                last.then_inc(prod_done, 1)

            def step(i, ahead):
                for q in range(TILES):
                    for g, n in groups:
                        if KINDS[g] == "A":
                            products(i, q, A_GROUPS.index((g, n)))
                        at = q * NG + g
                        if ahead > 1 and at == STAGE_AT:
                            stage_x0(i + 2)
                        if ahead > 1 and at == X0T_AT:
                            copy_x0t(i + 2)
                        if ahead > 0 and at == RELU_AT:
                            relu_x1(i + 1)
                            split_hi(i + 1, 0)
                if ahead > 0:
                    split_hi(i + 1, 1)

            act.wait_ge(w2_in, 16)
            nc.scalar.copy(w2_hi[:], w2[:]).then_inc(w2_hi_set, 1)
            act.wait_ge(rows_in, 16 * FIELDS)
            nc.scalar.copy(factor0_slot(KT, KS), factor0_rows(None, KS)).then_inc(near0_laid, 1)
            act.wait_ge(wrap_set, 1)
            for t in range(KT):
                if FAR0_BY[t] == "A":
                    n = k_rows[t] // FIELDS
                    nc.scalar.copy(factor0_slot(t, n), factor0_rows(KS * t, n)).then_inc(far0_laid_a, 1)
                if t == 1:
                    act.wait_ge(near0_full, 1)
                    nc.scalar.copy(near[:], x1_ps[0:KR, :]).then_inc(near0_set, 1)
                    stage_x0(1)
                if t == KT - 2:
                    copy_x0t(1)
            act.wait_ge(bias_in, 32)
            relu_x1(0)
            split_hi(0, 0)
            split_hi(0, 1)
            act.wait_ge(x0_ready, 1)
            step(0, 2)
            with nc.scalar.Fori(1, STEPS - 2) as i:
                step(i, 2)
            step(STEPS - 2, 1)
            step(STEPS - 1, 0)

            act.wait_ge(p2t_full, 1)
            nc.scalar.copy(p2_t[:], x1_ps[:]).then_inc(p2t_set, 1)
            act.wait_ge(mlp_in, 16 * 7)
            for c in range(C1):
                act.wait_ge(h1_full, c + 1)
                nc.scalar.activation(hid1[:, c, :], ya[c][:], ACT.Relu, bias=bt1[:, c:c + 1]).then_inc(h1_set, 1)
            for c in range(C2):
                act.wait_ge(h2_full, c + 1)
                nc.scalar.activation(hid2[:, c, :], yv[c][:], ACT.Relu, bias=bt2[:, c:c + 1]).then_inc(h2_set, 1)
            act.wait_ge(y_full, 1)
            nc.scalar.copy(y_sb[:], x1_ps[0:1, :]).then_inc(y_set, 1)

        @block.vector
        def _(dve):
            def multiply_pairs(i, t):
                n = k_rows[t]
                if isinstance(i, int) and i == 0:
                    if t == 0:
                        dve.wait_ge(near0_set, 1)
                    dve.wait_ge(far0_full, t + 1)
                    far_t = far0_banks[t % len(far0_banks)][0:n, :]
                else:
                    if t == 0:
                        dve.wait_ge(factors_in, i * (32 * KS))
                        dve.wait_ge(l1_done, i)
                    far_t = far[0:n, t, :]
                nc.vector.tensor_tensor(pairs[0:n, t, :], near[0:n, :], far_t, ALU.mult).then_inc(pairs_done, 1)

            def split_lo(i, part):
                cols = slice(0, NS - P) if part == 0 else slice(NS - P, NS)
                dve.wait_ge(hi_done, i * 2 + (part + 1))
                nc.vector.tensor_tensor(x1_lo[:, cols], x1[:, cols], x1_hi[:, cols], ALU.subtract).then_inc(lo_done, 1)

            def sum_x1(i):
                dve.wait_ge(x1_done, i + 1)
                nc.vector.tensor_reduce(p1[:, bass.ds(i * P, P)], x1[:].rearrange("s (q b) -> s b q", b=P),
                                        AX, ALU.add).then_inc(p1_done, 1)

            def mac_group(i, q, k, first):
                g, n = V_GROUPS[k]
                tile = i * TILES + q
                dve.wait_ge(yv_full, tile * NV + (k + 1))
                bank = yv[(q * NV + k) % V_RING]
                for j in range(n):
                    op = sum(m for _, m in V_GROUPS[:k]) + j
                    half = acc[:, q % 2, (op % 2) * S:(op % 2 + 1) * S]
                    y = bank[:, j * S:(j + 1) * S]
                    x = x0_scalar(i, q, GM * g + j)
                    if op == 0:
                        nc.vector.scalar_tensor_tensor(out=half, in0=y, scalar=x, in1=b2r[:], op0=ALU.mult,
                                                       op1=ALU.add).then_inc(macs, 1)
                    elif op == 1:
                        nc.vector.tensor_scalar(half, y, x, None, ALU.mult).then_inc(macs, 1)
                    else:
                        dve.wait_ge(macs, tile * V_OPS + (op - 1))
                        nc.vector.scalar_tensor_tensor(out=half, in0=y, scalar=x, in1=half, op0=ALU.mult,
                                                       op1=ALU.add).then_inc(macs, 1)
                    if (k, j) in FINISH_AT and not (first and q == 0):
                        part = FINISH_AT.index((k, j))
                        if q > 0:
                            finish_tile(i, q - 1, part)
                        else:
                            finish_tile(i - 1, TILES - 1, part)

            def finish_tile(i, q, part):
                tile = i * TILES + q
                begun = isinstance(i, int) and tile == 0
                if part == 0:
                    dve.wait_ge(added, (tile + 1) * ADDS)
                    dve.wait_ge(prod_done, (tile + 1) * NA)
                    if not begun:
                        dve.wait_ge(fold_d, tile)
                    nc.vector.tensor_tensor(fold[:], psum_g[:, q % 2, :], prod[:, NA - 1, :], ALU.add).then_inc(fold_a, 1)
                if part == 1:
                    dve.wait_ge(fold_a, tile + 1)
                    nc.vector.tensor_tensor(fold[:, 0:2 * S], fold[:, 0:2 * S], fold[:, 2 * S:4 * S], ALU.add).then_inc(fold_b, 1)
                if part == 2:
                    dve.wait_ge(fold_b, tile + 1)
                    dve.wait_ge(macs, (tile + 1) * V_OPS)
                    nc.vector.tensor_tensor(fold[:, 0:2 * S], fold[:, 0:2 * S], acc[:, q % 2, :], ALU.add).then_inc(fold_c, 1)
                if part == 3:
                    dve.wait_ge(fold_c, tile + 1)
                    if not begun:
                        dve.wait_ge(p2_done, tile)
                    nc.vector.tensor_tensor(total[:], fold[:, 0:S], fold[:, S:2 * S], ALU.add).then_inc(fold_d, 1)
                if part == 4:
                    dve.wait_ge(fold_d, tile + 1)
                    out = p2[:, bass.ds(i * S, S)]
                    if q == 0:
                        nc.vector.tensor_scalar(out, total[:], 0.0, None, ALU.max).then_inc(p2_done, 1)
                    else:
                        dve.wait_ge(p2_done, tile)
                        nc.vector.scalar_tensor_tensor(out=out, in0=total[:], scalar=0.0, in1=out, op0=ALU.max,
                                                       op1=ALU.add).then_inc(p2_done, 1)

            def step(i, first, ahead):
                for q in range(TILES):
                    for g, n in groups:
                        if KINDS[g] == "V":
                            mac_group(i, q, V_GROUPS.index((g, n)), first)
                        at = q * NG + g
                        if at == P1_AT:
                            sum_x1(i)
                        if ahead > 0 and at in PAIRS_AT:
                            multiply_pairs(i + 1, PAIRS_AT.index(at))
                        if ahead > 0 and at == LO_AT:
                            split_lo(i + 1, 0)
                if ahead > 0:
                    split_lo(i + 1, 1)

            dve.wait_ge(w1_in, 16 * 4)
            nc.vector.tensor_tensor(w1s[:, 0:KT - 1, :], w1f[:, 0:KT - 1, :], w1r[:, 0:KT - 1, :],
                                    ALU.add).then_inc(w1_fold, 1)
            dve.wait_ge(w1_fold, 1)
            nc.vector.tensor_copy(w1s[0:FIELDS, 0, :], w1f[0:FIELDS, 0, :])
            nc.vector.tensor_tensor(w1s[0:k_rows[-1], KT - 1, :], w1f[0:k_rows[-1], KT - 1, :],
                                    w1r[0:k_rows[-1], KT - 1, :], ALU.add).then_inc(w1_fold, 1)
            dve.wait_ge(w2_hi_set, 1)
            nc.vector.tensor_tensor(w2_lo[:], w2[:], w2_hi[:], ALU.subtract).then_inc(w2_lo_set, 1)
            dve.wait_ge(bias_in, 32)
            dve.wait_ge(rows_in, 16 * FIELDS)
            nc.vector.tensor_copy(rows[:, FIELDS * D:WIDE * D],
                                  rows[:, 0:(WIDE - FIELDS) * D]).then_inc(wrap_set, 1)
            dve.wait_ge(wrap_set, 1)
            for t in range(KT):
                if FAR0_BY[t] == "V":
                    n = k_rows[t] // FIELDS
                    nc.vector.tensor_copy(factor0_slot(t, n), factor0_rows(KS * t, n)).then_inc(far0_laid_v, 1)
            for t in range(KT):
                multiply_pairs(0, t)
            split_lo(0, 0)
            split_lo(0, 1)
            dve.wait_ge(x0_ready, 1)
            step(0, True, 1)
            with nc.vector.Fori(1, STEPS - 1) as i:
                step(i, False, 1)
            step(STEPS - 1, False, 0)
            for part in range(len(FINISH_AT)):
                finish_tile(STEPS - 1, TILES - 1, part)
            dve.wait_ge(p1_done, STEPS)
            nc.vector.tensor_reduce(p1_t[:].rearrange("s (k b) -> s k b", b=P),
                                    p1[:].rearrange("s (k j b) -> s k b j", k=BLOCKS, b=P),
                                    AX, ALU.add).then_inc(p_sums, 1)
            dve.wait_ge(p2_done, STEPS * TILES)
            nc.vector.tensor_reduce(p2_n[:], p2[:].rearrange("p (k j s) -> p k s j", k=BLOCKS, s=S),
                                    AX, ALU.add).then_inc(p_sums, 1)


def kernel(**inputs):
    import numpy as np
    import concourse.bacc as bacc
    from concourse import mybir as mb
    from concourse.bass_utils import run_bass_kernel_spmd

    fields = TABLES
    shifts = (fields + 1) // 2
    m = np.tile(np.arange(fields), shifts)
    far = (m + np.repeat(np.arange(shifts), fields)) % fields
    w1 = np.asarray(inputs["L0_rec_W1"])

    def columns(a):
        return np.asarray(a).reshape(-1, 128).T

    arrays = {
        "dense_t": np.asarray(inputs["dense_ctx"]).T,
        "ids": inputs["ids"],
        **{f"tbl_{f}": inputs[f"tbl_{f}"] for f in range(fields)},
        "w1_fwd": w1[:, m, far].T,
        "w1_rev": w1[:, far, m].T,
        "b1": inputs["L0_rec_b1"],
        "w2_t": np.asarray(inputs["L0_rec_W2"]).transpose(1, 2, 0).reshape(128, -1),
        "b2": inputs["L0_rec_b2"],
        "w_top1": inputs["W_top1"], "b_top1": columns(inputs["b_top1"]),
        "w_top2": inputs["W_top2"], "b_top2": columns(inputs["b_top2"]),
        "w_top3": columns(inputs["W_top3"]),
    }
    arrays = {k: np.ascontiguousarray(a) for k, a in arrays.items()}
    batch = arrays["ids"].shape[0]
    nc = bacc.Bacc("TRN2", target_bir_lowering=False, num_devices=1)
    aps = {k: nc.dram_tensor(k, a.shape, mb.dt.from_np(a.dtype), kind="ExternalInput").ap() for k, a in arrays.items()}
    tables = [aps.pop(f"tbl_{f}") for f in range(fields)]
    y_out = nc.dram_tensor("y_out", (batch, 1), mb.dt.float32, kind="ExternalOutput").ap()
    build_tower(nc, tables=tables, y_out=y_out, **aps)
    result = run_bass_kernel_spmd(nc, [arrays], core_ids=[0])
    return result.results[0]["y_out"]
```

```python
import concourse.bass as bass
from concourse import mybir
from contextlib import ExitStack

TABLES = 39


def build_tower(nc, dense_t, ids_t, field_base, table, w1_fwd, w1_rev, b1, w2_t, b2, w_top1, b_top1, w_top2,
                b_top2, w_top3, y_out):
    F32, F32R, I32 = mybir.dt.float32, mybir.dt.float32r, mybir.dt.int32
    ALU = mybir.AluOpType
    ACT = mybir.ActivationFunctionType
    AXES = mybir.AxisListType.XY
    P = 128

    FIELDS = TABLES
    D = table.shape[1]
    S = b1.shape[0]
    BATCH = y_out.shape[0]
    TILES = 4
    NS = TILES * P
    SB = NS // D
    TD = D // TILES
    STEPS = BATCH // SB
    LEAD = 3
    GF = P // SB
    GATHERS = -(-FIELDS // GF)
    g_rows = [min(P, (FIELDS - GF * j) * SB) for j in range(GATHERS)]
    SHIFTS = (FIELDS + 1) // 2
    PAIRS = FIELDS * SHIFTS
    KS = P // FIELDS
    KR = KS * FIELDS
    KT = -(-SHIFTS // KS)
    k_rows = [min(KR, PAIRS - KR * t) for t in range(KT)]
    WIDE = FIELDS + SHIFTS - 1
    STORES = sum((n >= GF) + (n % GF > 0) for n in (FIELDS, WIDE - FIELDS))
    FAR_EARLY = 2
    STEP_X0 = FIELDS * TILES

    GM = 4
    KINDS = "AVAVAAVAAV"
    NG = len(KINDS)
    groups = [(g, min(GM, FIELDS - GM * g)) for g in range(NG)]
    V_GROUPS = [x for x in groups if KINDS[x[0]] == "V"]
    A_GROUPS = [x for x in groups if KINDS[x[0]] == "A"]
    NV, NA = len(V_GROUPS), len(A_GROUPS)
    V_OPS = sum(n for _, n in V_GROUPS)
    ADDS = NA - 2
    V_RING, A_RING = 2, 4
    assert (TILES * NV) % V_RING == 0 and (TILES * NA) % A_RING == 0
    assert KINDS[-1] == "V" and GM * NG >= FIELDS and all(n == GM for _, n in A_GROUPS)

    T_AT = 23
    X0_AT = T_AT + 2
    P2_AT = 14
    P2T_AT = P2_AT + 2
    L1_AT = [12, 14, 18, 22, 25, 28, 32]
    PAIRS_AT = [6, 9, 11, 16, 21, 24, 27]
    RELU_AT = L1_AT[-1] + 1
    LO_AT = RELU_AT + 2
    P1_AT = 9
    FINISH_AT = [(1, 3), (2, 1), (2, 3), (3, 0), (3, 2)]
    LAST_FINISH_AT = [(1, 3), (2, 0), (2, 1), (2, 2), (2, 3)]
    GATHER_FROM = 3

    MLP_AT = [21, 23, 26, 29, 32, 35, 38]
    RELUS_AT = [21, 24, 27, 30, 33, 36, 39]
    LOWS_AT = [at + 1 for at in RELUS_AT[:4]]
    P1_HI_AT, P1_LO_AT = 5, 8
    P2_LO_AT = P2T_AT + 1

    HID1, HID2 = w_top1.shape[1], w_top2.shape[1]
    C1, C2 = HID1 // P, HID2 // P
    DENSE = dense_t.shape[0]
    assert len(MLP_AT) == C1 + C2 + 1 and C1 == A_RING and C2 == 2
    NF = BATCH - SB
    FRONT, LAST = slice(0, NF), slice(NF, BATCH)

    ctx = ExitStack()
    with ctx:
        def sb(name, shape, dt=F32):
            return ctx.enter_context(nc.sbuf_tensor(name, shape, dt))

        def pb(name, shape):
            return ctx.enter_context(nc.psum_tensor(name, shape, F32))

        def sem(name):
            return ctx.enter_context(nc.semaphore(name))

        ids_in_sb = sb("ids_in_sb", [P, STEPS * GATHERS], I32)
        base_sb = sb("base_sb", [P, STEPS * GATHERS], I32)
        ids_sb = sb("ids_sb", [P, STEPS * GATHERS], I32)
        ids_step = sb("ids_step", [P, GATHERS], I32)
        rows_first = sb("rows_first", [P, GATHERS * D])
        rows_second = sb("rows_second", [P, GATHERS * D])
        scratch = nc.dram_tensor("x0_scratch", (STEPS, WIDE, NS), F32, kind="Internal").ap()
        x0 = sb("x0", [P, STEPS * STEP_X0])
        near = sb("near", [KR, NS])
        far = sb("far", [KR, KT, NS])
        pairs = sb("pairs", [KR, KT, NS])
        ident = sb("ident", [P, P])
        ones = sb("ones", [P, P])
        sel_low = sb("sel_low", [P, SB])
        sel = sb("sel", [P, SB])
        w1s = sb("w1s", [KR, KT, S])
        w1r = sb("w1r", [KR, KT, S])
        w2 = sb("w2", [S, FIELDS * S])
        w2_hi = sb("w2_hi", [S, FIELDS * S], F32R)
        w2_lo = sb("w2_lo", [S, FIELDS * S], F32R)
        b1c = sb("b1c", [S, 1])
        b2r = sb("b2r", [P, S])
        x1 = sb("x1", [S, NS])
        x1_hi = sb("x1_hi", [S, NS], F32R)
        x1_lo = sb("x1_lo", [S, NS], F32R)
        prod = sb("prod", [P, NA, GM * S])
        pool_sum = sb("pool_sum", [P, 2, GM * S])
        acc = sb("acc", [P, 2, 2 * S])
        fold = sb("fold", [P, GM * S])
        total = sb("total", [P, S])
        p2 = sb("p2", [P, 2, S])
        p1_t = sb("p1_t", [S, BATCH])
        p2_t = sb("p2_t", [S, BATCH])
        dense = sb("dense", [DENSE, BATCH])
        wt1 = sb("wt1", [P, 2, HID1])
        wt1_dense = sb("wt1_dense", [DENSE, HID1])
        wt2 = sb("wt2", [P, C1, HID2])
        wt3 = sb("wt3", [P, C2])
        bt1 = sb("bt1", [P, C1])
        bt2 = sb("bt2", [P, C2])
        hid1 = w2[:, 0:2 * NF].rearrange("p (c n) -> p c n", c=2)
        hid1_last = sb("hid1_last", [P, C1, SB])
        wt1_hi = sb("wt1_hi", [P, 2, HID1], F32R)
        wt1_lo = sb("wt1_lo", [P, 2, HID1], F32R)
        wt1_dense_hi = sb("wt1_dense_hi", [DENSE, HID1], F32R)
        wt1_dense_lo = sb("wt1_dense_lo", [DENSE, HID1], F32R)
        wt2_hi = sb("wt2_hi", [P, C1, HID2], F32R)
        wt2_lo = sb("wt2_lo", [P, C1, HID2], F32R)
        dense_hi = sb("dense_hi", [DENSE, NF], F32R)
        dense_lo = sb("dense_lo", [DENSE, NF], F32R)
        p_hi = sb("p_hi", [S, 2, NF], F32R)
        p_lo = sb("p_lo", [S, 2, NF], F32R)
        hid1_hi = sb("hid1_hi", [P, C1, NF], F32R)
        hid1_lo = sb("hid1_lo", [P, C1, NF], F32R)
        hid2 = w2[:, 2 * NF:2 * NF + C2 * BATCH].rearrange("p (c n) -> p c n", c=C2)
        y_sb = w2[0:1, 2 * NF + C2 * BATCH:2 * NF + (C2 + 1) * BATCH]

        yv = [pb(f"yv{i}", [P, GM * S]) for i in range(V_RING)]
        ya = [pb(f"ya{i}", [P, GM * S]) for i in range(A_RING)]
        x1_ps = pb("x1_ps", [P, NS])
        side_ps = pb("side_ps", [P, NS])
        x0_ps = side_ps[:, 0:TILES * KR]
        mlp_banks = (x1_ps, side_ps)
        p2_ps = side_ps[:, NS - SB:NS]

        ids_in = sem("ids_in")
        w1_in = sem("w1_in")
        w2_in = sem("w2_in")
        bias_in = sem("bias_in")
        mlp_in = sem("mlp_in")
        wt2_in = sem("wt2_in")
        ones_set = sem("ones_set")
        ident_set = sem("ident_set")
        ids_based = sem("ids_based")
        ids_staged = sem("ids_staged")
        rows_in = sem("rows_in")
        rows1_in = sem("rows1_in")
        w1_fold = sem("w1_fold")
        w2_hi_set = sem("w2_hi_set")
        w2_lo_set = sem("w2_lo_set")
        sel_low_set = sem("sel_low_set")
        sel_set = sem("sel_set")
        scratch_in = sem("scratch_in")
        near_in = sem("near_in")
        far_in = sem("far_in")
        x0_full = sem("x0_full")
        x0_set = sem("x0_set")
        pairs_done = sem("pairs_done")
        factors_used = sem("factors_used")
        l1_done = sem("l1_done")
        x1_done = sem("x1_done")
        hi_done = sem("hi_done")
        lo_done = sem("lo_done")
        p1_done = sem("p1_done")
        ya_full = sem("ya_full")
        yv_full = sem("yv_full")
        prod_done = sem("prod_done")
        added = sem("added")
        macs = sem("macs")
        fold_a = sem("fold_a")
        fold_b = sem("fold_b")
        fold_c = sem("fold_c")
        fold_d = sem("fold_d")
        p2_done = sem("p2_done")
        p2_full = sem("p2_full")
        p2_set = sem("p2_set")
        mlp_hi_set = sem("mlp_hi_set")
        mlp_lo_set = sem("mlp_lo_set")
        p_hi_set = sem("p_hi_set")
        p_lo_set = sem("p_lo_set")
        h1_hi = sem("h1_hi")
        h1_lo = sem("h1_lo")
        h1_full = sem("h1_full")
        h1_set = sem("h1_set")
        h1_last_a = sem("h1_last_a")
        h1_last_v = sem("h1_last_v")
        h2_full = sem("h2_full")
        h2_set = sem("h2_set")
        h2_last_a = sem("h2_last_a")
        h2_last_v = sem("h2_last_v")
        y_full = sem("y_full")
        y_set = sem("y_set")
        y_stored = sem("y_stored")

        def x0_scalar(i, q, m):
            return x0[:, bass.ds(i * STEP_X0 + (q * FIELDS + m), 1)]

        def x1_part(i, part):
            at = P if isinstance(i, int) and i == 0 else NS - P
            return slice(0, at) if part == 0 else slice(at, NS)

        def w2_cols(w, g, n):
            return w[:, GM * g * S:(GM * g + n) * S]

        block = ctx.enter_context(nc.Block())

        @block.sync
        def _(sp):
            sp.dma_start(ids_in_sb[:], ids_t).then_inc(ids_in, 16)
            sp.dma_start(base_sb[:], field_base).then_inc(ids_in, 16)
            full = KR * (KT - 1)
            for dst, src in ((w1s, w1_fwd), (w1r, w1_rev)):
                sp.dma_start(dst[:, 0:KT - 1, :],
                             src[0:full, :].rearrange("(t p) s -> p t s", p=KR)).then_inc(w1_in, 16)
                sp.dma_start(dst[0:k_rows[-1], KT - 1, :], src[full:PAIRS, :]).then_inc(w1_in, 16)
            sp.dma_start(b1c[:], b1.rearrange("(s a) -> s a", a=1)).then_inc(bias_in, 16)
            sp.dma_start(b2r[:], b2.partition_broadcast(P)).then_inc(bias_in, 16)
            sp.dma_start(w2[:], w2_t).then_inc(w2_in, 16)
            sp.dma_start(dense[:], dense_t).then_inc(mlp_in, 16)
            sp.dma_start(wt1[:], w_top1[0:2 * P, :].rearrange("(k p) n -> p k n", p=P)).then_inc(mlp_in, 16)
            sp.dma_start(wt1_dense[:], w_top1[2 * P:2 * P + DENSE, :]).then_inc(mlp_in, 16)
            sp.dma_start(wt3[:], w_top3).then_inc(mlp_in, 16)
            sp.dma_start(bt1[:], b_top1).then_inc(mlp_in, 16)
            sp.dma_start(bt2[:], b_top2).then_inc(mlp_in, 16)

            def store_rows(i, rows):
                if isinstance(i, int) and i == 1:
                    sp.wait_ge(rows1_in, 16 * GATHERS)
                elif isinstance(i, int) and i == 0:
                    sp.wait_ge(rows_in, 16 * GATHERS)
                else:
                    sp.wait_ge(rows_in, i * (16 * GATHERS))
                base = i * (WIDE * NS)
                for at, n in ((0, FIELDS), (FIELDS, WIDE - FIELDS)):
                    whole, left = n // GF, n % GF
                    if whole:
                        to = bass.AP(scratch.tensor, base + at * NS, [[D, P], [P * D, whole], [1, D]])
                        sp.dma_start(to, rows[:, 0:whole * D].rearrange("p (j d) -> p j d", d=D)
                                     ).then_inc(scratch_in, 16)
                    if left:
                        to = bass.AP(scratch.tensor, base + (at + whole * GF) * NS, [[D, left * SB], [1, D]])
                        sp.dma_start(to, rows[0:left * SB, whole * D:(whole + 1) * D]).then_inc(scratch_in, 16)

            def spread_factors(i):
                sp.wait_ge(scratch_in, (i + 1) * (16 * STORES))
                if not (isinstance(i, int) and i == 0):
                    sp.wait_ge(factors_used, i)
                    sp.wait_ge(x0_full, i)
                base = i * (WIDE * NS)

                def load(to, n, shift, stride, loaded):
                    rows = bass.AP(scratch.tensor, base + shift * NS, [[stride, n], [NS, FIELDS], [1, NS]])
                    sp.dma_start(to, rows).then_inc(loaded, 16)

                load(near[:], KS, 0, 0, near_in)
                for t in range(KT):
                    load(far[0:k_rows[t], t, :], k_rows[t] // FIELDS, KS * t, NS,
                         near_in if t < FAR_EARLY else far_in)

            store_rows(0, rows_first)
            spread_factors(0)
            sp.dma_start(wt2[:], w_top2.rearrange("(k p) n -> p k n", p=P)).then_inc(wt2_in, 16)
            store_rows(1, rows_second)
            spread_factors(1)
            store_rows(2, rows_first)
            with nc.sync.Fori(2, STEPS - 1) as i:
                spread_factors(i)
                store_rows(i + 1, rows_second)
            spread_factors(STEPS - 1)
            sp.wait_ge(y_set, 2)
            sp.dma_start(y_out.rearrange("b a -> a b"), y_sb).then_inc(y_stored, 16)
            sp.wait_ge(y_stored, 16)

        @block.gpsimd
        def _(pool):
            def stage_ids(i):
                pool.wait_ge(scratch_in, i * (16 * STORES))
                nc.gpsimd.tensor_copy(ids_step[:], ids_sb[:, bass.ds(i * GATHERS, GATHERS)]).then_inc(ids_staged, 1)

            def gather(j, ids, rows, done=rows_in):
                n = g_rows[j]
                nc.gpsimd.indirect_dma_start(
                    out=rows[0:n, j * D:(j + 1) * D], out_offset=None, in_=table,
                    in_offset=bass.IndirectOffsetOnAxis(ap=ids[0:n, j:j + 1], axis=0)).then_inc(done, 16)

            def step(i, ahead):
                for q in range(TILES):
                    tile = i * TILES + q
                    out = pool_sum[:, q % 2, :]
                    for j in range(ADDS):
                        at = q * ADDS + j - GATHER_FROM
                        if ahead and at == 0:
                            stage_ids(i + LEAD)
                        pool.wait_ge(prod_done, tile * NA + (j + 2))
                        if j == 0:
                            if not (isinstance(i, int) and i == 0 and q < 2):
                                pool.wait_ge(fold_a, tile - 1)
                            before = prod[:, 0, :]
                        else:
                            pool.wait_ge(added, tile * ADDS + j)
                            before = out
                        if ahead and at == 0:
                            pool.wait_ge(ids_staged, i + 1)
                        nc.gpsimd.tensor_tensor(out, before, prod[:, j + 1, :], ALU.add).then_inc(added, 1)
                        slots = TILES * ADDS - GATHER_FROM
                        if ahead and at >= 0:
                            for k in range(at * GATHERS // slots, (at + 1) * GATHERS // slots):
                                gather(k, ids_step, rows_second)

            pool.wait_ge(ids_in, 32)
            nc.gpsimd.tensor_tensor(ids_sb[:], ids_in_sb[:], base_sb[:], ALU.add).then_inc(ids_based, 1)
            pool.wait_ge(ids_based, 1)
            for i in range(LEAD):
                if i == 2:
                    pool.wait_ge(scratch_in, 16 * STORES)
                for k in range(GATHERS):
                    if i == 1:
                        gather(k, ids_sb[:, i * GATHERS:(i + 1) * GATHERS], rows_second, rows1_in)
                    else:
                        gather(k, ids_sb[:, i * GATHERS:(i + 1) * GATHERS], rows_first)
                if i == 0:
                    nc.gpsimd.memset(ones[:], 1.0).then_inc(ones_set, 1)
                    pool.wait_ge(ones_set, 1)
                    nc.gpsimd.affine_select(out=ident[:], in_=ones[:], compare_op=ALU.is_equal, fill=0.0, base=0,
                                            pattern=[[-1, P]], channel_multiplier=1).then_inc(ident_set, 1)
                    nc.gpsimd.affine_select(out=sel_low[:], in_=ones[:, 0:SB], compare_op=ALU.is_ge, fill=0.0,
                                            base=0, pattern=[[-TD, SB]], channel_multiplier=1).then_inc(sel_low_set, 1)
                    pool.wait_ge(sel_low_set, 1)
                    nc.gpsimd.affine_select(out=sel[:], in_=sel_low[:], compare_op=ALU.is_ge, fill=0.0,
                                            base=TD - 1, pattern=[[TD, SB]], channel_multiplier=-1).then_inc(sel_set, 1)
            step(0, True)
            with nc.gpsimd.Fori(1, STEPS - LEAD) as i:
                step(i, True)
            with nc.gpsimd.Fori(STEPS - LEAD, STEPS) as i:
                step(i, False)

        @block.tensor
        def _(pe):
            def transpose_x0(i):
                pe.wait_ge(near_in, (i + 1) * (16 * (1 + FAR_EARLY)))
                if not (isinstance(i, int) and i <= 1):
                    pe.wait_ge(p2_set, i - 1)
                for q in range(TILES):
                    last = nc.tensor.transpose(x0_ps[:, q * KR:(q + 1) * KR], near[:, q::TILES],
                                               ident[0:KR, 0:KR])
                last.then_inc(x0_full, 1)

            def sum_p2(i):
                pe.wait_ge(p2_done, (i + 1) * TILES)
                nc.tensor.matmul(p2_ps, p2[:, (TILES - 1) % 2, :], sel[:], start=True, stop=True).then_inc(p2_full, 1)

            def layer1(i, t):
                if t < KT - 1:
                    pe.wait_ge(pairs_done, i * (KT - 1) + (t + 1))
                else:
                    pe.wait_ge(factors_used, i + 1)
                if t == 0 and not (isinstance(i, int) and i == 0):
                    pe.wait_ge(x1_done, i)
                n = k_rows[t]
                last = nc.tensor.matmul(x1_ps[:], w1s[0:n, t, :], pairs[0:n, t, :],
                                        start=(t == 0), stop=(t == KT - 1))
                if t == KT - 1:
                    last.then_inc(l1_done, 1)

            def layer2(i, q, g, n):
                tile = i * TILES + q
                static = isinstance(i, int)
                if KINDS[g] == "V":
                    k = V_GROUPS.index((g, n))
                    if not (static and tile * NV + k < V_RING):
                        back = k - V_RING
                        done = sum(m for _, m in V_GROUPS[:back % NV + 1]) + (back // NV) * V_OPS
                        pe.wait_ge(macs, tile * V_OPS + done)
                    bank, full = yv[(q * NV + k) % V_RING], yv_full
                else:
                    k = A_GROUPS.index((g, n))
                    if not (static and tile * NA + k < A_RING):
                        pe.wait_ge(prod_done, tile * NA + (k - A_RING + 1))
                    bank, full = ya[(q * NA + k) % A_RING], ya_full
                out = bank[:, 0:n * S]
                hi, lo = x1_hi[:, q * P:(q + 1) * P], x1_lo[:, q * P:(q + 1) * P]
                nc.tensor.matmul(out, hi, w2_cols(w2_hi, g, n), start=True, stop=False)
                nc.tensor.matmul(out, hi, w2_cols(w2_lo, g, n), start=False, stop=False)
                nc.tensor.matmul(out, lo, w2_cols(w2_hi, g, n), start=False, stop=True).then_inc(full, 1)

            def halves(out, w_hi, w_lo, x_hi, x_lo, start, stop):
                nc.tensor.matmul(out, w_hi, x_hi, start=start, stop=False)
                nc.tensor.matmul(out, w_lo, x_hi, start=False, stop=False)
                return nc.tensor.matmul(out, w_hi, x_lo, start=False, stop=stop)

            def hidden1(out, c, rows_of, start, stop):
                for k, (w, x) in enumerate(rows_of):
                    last = nc.tensor.matmul(out, w[:, c * P:(c + 1) * P], x, start=start and k == 0,
                                            stop=stop and k == len(rows_of) - 1)
                return last

            def front_mlp(u):
                out = mlp_banks[u % 2][:, 0:NF]
                if u < C1:
                    cols = slice(u * P, (u + 1) * P)
                    if u == 0:
                        pe.wait_ge(x1_done, STEPS)
                        pe.wait_ge(mlp_lo_set, 1)
                        pe.wait_ge(p_lo_set, 2)
                    if u >= 2:
                        pe.wait_ge(h1_set, u - 1)
                    halves(out, wt1_dense_hi[:, cols], wt1_dense_lo[:, cols], dense_hi[:], dense_lo[:], True, False)
                    for k in range(2):
                        last = halves(out, wt1_hi[:, k, cols], wt1_lo[:, k, cols], p_hi[:, k, :], p_lo[:, k, :],
                                      False, k == 1)
                    last.then_inc(h1_full, 1)
                elif u < C1 + C2:
                    c = u - C1
                    cols = slice(c * P, (c + 1) * P)
                    pe.wait_ge(h1_set, u - 1)
                    for k in range(C1):
                        if c == 0:
                            pe.wait_ge(h1_lo, k + 1)
                        last = halves(out, wt2_hi[:, k, cols], wt2_lo[:, k, cols], hid1_hi[:, k, :],
                                      hid1_lo[:, k, :], k == 0, k == C1 - 1)
                    last.then_inc(h2_full, 1)
                else:
                    pe.wait_ge(h2_set, C2)
                    for k in range(C2):
                        last = nc.tensor.matmul(out[0:1, :], wt3[:, k:k + 1], hid2[:, k, FRONT],
                                                start=(k == 0), stop=(k == C2 - 1))
                    last.then_inc(y_full, 1)

            def last_mlp():
                pe.wait_ge(p1_done, STEPS)
                for c in range(C1):
                    pe.wait_ge(prod_done, STEPS * TILES * NA - (A_RING - 1 - c))
                    hidden1(ya[c][:, 0:SB], c, ((wt1[:, 0, :], p1_t[:, LAST]), (wt1_dense, dense[:, LAST])),
                            True, False)
                sum_p2(STEPS - 1)
                pe.wait_ge(p2_set, STEPS)
                for c in range(C1):
                    hidden1(ya[c][:, 0:SB], c, ((wt1[:, 1, :], p2_t[:, LAST]),), False, True).then_inc(h1_full, 1)
                pe.wait_ge(y_set, 1)
                for k in range(C1):
                    if k % 2 == 0:
                        pe.wait_ge(h1_last_a, k // 2 + 1)
                    else:
                        pe.wait_ge(h1_last_v, k // 2 + 1)
                    for c in range(C2):
                        last = nc.tensor.matmul((x1_ps, yv[0])[c][:, 0:SB], wt2[:, k, c * P:(c + 1) * P],
                                                hid1_last[:, k, :], start=(k == 0), stop=(k == C1 - 1))
                        if k == C1 - 1:
                            last.then_inc(h2_full, 1)
                for k in range(C2):
                    if k % 2 == 0:
                        pe.wait_ge(h2_last_a, k // 2 + 1)
                    else:
                        pe.wait_ge(h2_last_v, k // 2 + 1)
                    last = nc.tensor.matmul(yv[1][0:1, 0:SB], wt3[:, k:k + 1], hid2[:, k, LAST],
                                            start=(k == 0), stop=(k == C2 - 1))
                last.then_inc(y_full, 1)

            def step(i, ahead):
                first = isinstance(i, int) and i == 0
                for q in range(TILES):
                    if q == 0:
                        pe.wait_ge(lo_done, i * 2 + 1)
                    if q == (1 if first else TILES - 1):
                        pe.wait_ge(lo_done, i * 2 + 2)
                    for g, n in groups:
                        layer2(i, q, g, n)
                        at = q * NG + g
                        if at == P2_AT and not first:
                            pe.wait_ge(x0_set, i + 1)
                            sum_p2(i - 1)
                        if ahead and at == T_AT:
                            transpose_x0(i + 1)
                        if ahead and at in L1_AT:
                            layer1(i + 1, L1_AT.index(at))
                        if not ahead and at in MLP_AT:
                            front_mlp(MLP_AT.index(at))

            pe.wait_ge(ident_set, 1)
            pe.wait_ge(sel_set, 1)
            transpose_x0(0)
            pe.wait_ge(w1_fold, 2)
            for t in range(KT):
                layer1(0, t)
            pe.wait_ge(w2_hi_set, 1)
            pe.wait_ge(w2_lo_set, 1)
            step(0, True)
            with nc.tensor.Fori(1, STEPS - 1) as i:
                step(i, True)
            step(STEPS - 1, False)
            last_mlp()

        @block.scalar
        def _(act):
            def copy_x0(i):
                act.wait_ge(x0_full, i + 1)
                nc.scalar.copy(x0[:, bass.ds(i * STEP_X0, STEP_X0)].rearrange("p (q m) -> p q m", q=TILES),
                               x0_ps.rearrange("p (q m) -> p q m", q=TILES)[:, :, 0:FIELDS]).then_inc(x0_set, 1)

            def copy_p2(i):
                act.wait_ge(p2_full, i + 1)
                nc.scalar.copy(p2_t[:, bass.ds(i * SB, SB)], p2_ps).then_inc(p2_set, 1)

            def relu_x1(i):
                act.wait_ge(l1_done, i + 1)
                if not (isinstance(i, int) and i == 0):
                    act.wait_ge(lo_done, i * 2)
                    act.wait_ge(p1_done, i)
                nc.scalar.activation(x1[:].rearrange("s (q k) -> s q k", q=TILES),
                                     x1_ps[:].rearrange("s (k q) -> s q k", q=TILES), ACT.Relu,
                                     bias=b1c[:, 0:1]).then_inc(x1_done, 1)

            def split_hi(i, part):
                cols = x1_part(i, part)
                act.wait_ge(x1_done, i + 1)
                if not (isinstance(i, int) and i == 0):
                    act.wait_ge(yv_full, i * (TILES * NV) - (NV if part == 0 else 0))
                nc.scalar.copy(x1_hi[:, cols], x1[:, cols]).then_inc(hi_done, 1)

            def products(i, q, k):
                g, n = A_GROUPS[k]
                tile = i * TILES + q
                act.wait_ge(ya_full, tile * NA + (k + 1))
                if not (isinstance(i, int) and tile == 0):
                    if k <= ADDS:
                        act.wait_ge(added, (tile - 1) * ADDS + max(k, 1))
                    else:
                        act.wait_ge(fold_a, tile)
                bank = ya[(q * NA + k) % A_RING]
                for j in range(n):
                    last = nc.scalar.activation(prod[:, k, j * S:(j + 1) * S], bank[:, j * S:(j + 1) * S],
                                                ACT.Copy, scale=x0_scalar(i, q, GM * g + j))
                last.then_inc(prod_done, 1)

            def front_mlp(u):
                out = mlp_banks[u % 2][:, 0:NF]
                if u < C1:
                    act.wait_ge(h1_full, u + 1)
                    if u >= 2:
                        act.wait_ge(h1_lo, u - 1)
                    nc.scalar.activation(hid1[:, u % 2, :], out, ACT.Relu,
                                         bias=bt1[:, u:u + 1]).then_inc(h1_set, 1)
                    act.wait_ge(h1_set, u + 1)
                    nc.scalar.copy(hid1_hi[:, u, :], hid1[:, u % 2, :]).then_inc(h1_hi, 1)
                elif u < C1 + C2:
                    c = u - C1
                    act.wait_ge(h2_full, c + 1)
                    nc.scalar.activation(hid2[:, c, FRONT], out, ACT.Relu,
                                         bias=bt2[:, c:c + 1]).then_inc(h2_set, 1)
                else:
                    act.wait_ge(y_full, 1)
                    nc.scalar.copy(y_sb[:, FRONT], out[0:1, :]).then_inc(y_set, 1)

            def last_mlp():
                copy_p2(STEPS - 1)
                for c in range(0, C1, 2):
                    act.wait_ge(h1_full, C1 + c + 1)
                    nc.scalar.activation(hid1_last[:, c, :], ya[c][:, 0:SB], ACT.Relu,
                                         bias=bt1[:, c:c + 1]).then_inc(h1_last_a, 1)
                for c in range(0, C2, 2):
                    act.wait_ge(h2_full, C2 + c + 1)
                    nc.scalar.activation(hid2[:, c, LAST], (x1_ps, yv[0])[c][:, 0:SB], ACT.Relu,
                                         bias=bt2[:, c:c + 1]).then_inc(h2_last_a, 1)
                act.wait_ge(y_full, 2)
                nc.scalar.copy(y_sb[:, LAST], yv[1][0:1, 0:SB]).then_inc(y_set, 1)

            def step(i, ahead):
                for q in range(TILES):
                    for g, n in groups:
                        if KINDS[g] == "A":
                            products(i, q, A_GROUPS.index((g, n)))
                        at = q * NG + g
                        if ahead and at == X0_AT:
                            copy_x0(i + 1)
                        if at == P2T_AT and not (isinstance(i, int) and i == 0):
                            copy_p2(i - 1)
                            if not ahead:
                                act.wait_ge(p2_set, STEPS - 1)
                                nc.scalar.copy(p_hi[:, 1, :], p2_t[:, FRONT]).then_inc(p_hi_set, 1)
                        if not ahead and at == P1_HI_AT:
                            act.wait_ge(p1_done, STEPS - 1)
                            nc.scalar.copy(p_hi[:, 0, :], p1_t[:, FRONT]).then_inc(p_hi_set, 1)
                        if ahead and at == RELU_AT:
                            relu_x1(i + 1)
                            split_hi(i + 1, 0)
                        if not ahead and at in RELUS_AT:
                            front_mlp(RELUS_AT.index(at))
                if ahead:
                    split_hi(i + 1, 1)

            act.wait_ge(w2_in, 16)
            nc.scalar.copy(w2_hi[:], w2[:]).then_inc(w2_hi_set, 1)
            act.wait_ge(mlp_in, 16 * 6)
            nc.scalar.copy(wt1_hi[:], wt1[:])
            nc.scalar.copy(wt1_dense_hi[:], wt1_dense[:])
            nc.scalar.copy(dense_hi[:], dense[:, FRONT]).then_inc(mlp_hi_set, 1)
            act.wait_ge(bias_in, 32)
            copy_x0(0)
            act.wait_ge(wt2_in, 16)
            nc.scalar.copy(wt2_hi[:], wt2[:]).then_inc(mlp_hi_set, 1)
            relu_x1(0)
            split_hi(0, 0)
            split_hi(0, 1)
            step(0, True)
            with nc.scalar.Fori(1, STEPS - 1) as i:
                step(i, True)
            step(STEPS - 1, False)
            last_mlp()

        @block.vector
        def _(dve):
            def multiply_pairs(i, t):
                if t == 0:
                    dve.wait_ge(near_in, (i + 1) * (16 * (1 + FAR_EARLY)))
                    if not (isinstance(i, int) and i == 0):
                        dve.wait_ge(l1_done, i)
                if t == FAR_EARLY:
                    dve.wait_ge(far_in, (i + 1) * (16 * (KT - FAR_EARLY)))
                n = k_rows[t]
                nc.vector.tensor_tensor(pairs[0:n, t, :], near[0:n, :], far[0:n, t, :],
                                        ALU.mult).then_inc(pairs_done if t < KT - 1 else factors_used, 1)

            def split_lo(i, part):
                cols = x1_part(i, part)
                dve.wait_ge(hi_done, i * 2 + (part + 1))
                nc.vector.tensor_tensor(x1_lo[:, cols], x1[:, cols], x1_hi[:, cols], ALU.subtract).then_inc(lo_done, 1)

            def sum_x1(i):
                dve.wait_ge(x1_done, i + 1)
                nc.vector.tensor_reduce(p1_t[:, bass.ds(i * SB, SB)], x1[:].rearrange("s (q b e) -> s b q e", q=TILES, e=TD),
                                        AXES, ALU.add).then_inc(p1_done, 1)

            def mac_group(i, q, k, first, finish_at=FINISH_AT):
                g, n = V_GROUPS[k]
                tile = i * TILES + q
                dve.wait_ge(yv_full, tile * NV + (k + 1))
                bank = yv[(q * NV + k) % V_RING]
                for j in range(n):
                    op = sum(m for _, m in V_GROUPS[:k]) + j
                    half = acc[:, q % 2, (op % 2) * S:(op % 2 + 1) * S]
                    y = bank[:, j * S:(j + 1) * S]
                    x = x0_scalar(i, q, GM * g + j)
                    if op == 0:
                        nc.vector.scalar_tensor_tensor(out=half, in0=y, scalar=x, in1=b2r[:], op0=ALU.mult,
                                                       op1=ALU.add).then_inc(macs, 1)
                    elif op == 1:
                        nc.vector.tensor_scalar(half, y, x, None, ALU.mult).then_inc(macs, 1)
                    else:
                        dve.wait_ge(macs, tile * V_OPS + (op - 1))
                        nc.vector.scalar_tensor_tensor(out=half, in0=y, scalar=x, in1=half, op0=ALU.mult,
                                                       op1=ALU.add).then_inc(macs, 1)
                    if (k, j) in finish_at and not (first and q == 0):
                        part = finish_at.index((k, j))
                        if q > 0:
                            finish_tile(i, q - 1, part)
                        else:
                            finish_tile(i - 1, TILES - 1, part)

            def finish_tile(i, q, part):
                tile = i * TILES + q
                begun = isinstance(i, int) and tile == 0
                if part == 0:
                    dve.wait_ge(added, (tile + 1) * ADDS)
                    dve.wait_ge(prod_done, (tile + 1) * NA)
                    if not begun:
                        dve.wait_ge(fold_d, tile)
                    nc.vector.tensor_tensor(fold[:], pool_sum[:, q % 2, :], prod[:, NA - 1, :], ALU.add).then_inc(fold_a, 1)
                if part == 1:
                    dve.wait_ge(fold_a, tile + 1)
                    nc.vector.tensor_tensor(fold[:, 0:2 * S], fold[:, 0:2 * S], fold[:, 2 * S:4 * S], ALU.add).then_inc(fold_b, 1)
                if part == 2:
                    dve.wait_ge(fold_b, tile + 1)
                    dve.wait_ge(macs, (tile + 1) * V_OPS)
                    nc.vector.tensor_tensor(fold[:, 0:2 * S], fold[:, 0:2 * S], acc[:, q % 2, :], ALU.add).then_inc(fold_c, 1)
                if part == 3:
                    dve.wait_ge(fold_c, tile + 1)
                    if not begun:
                        dve.wait_ge(p2_done, tile)
                    nc.vector.tensor_tensor(total[:], fold[:, 0:S], fold[:, S:2 * S], ALU.add).then_inc(fold_d, 1)
                if part == 4:
                    dve.wait_ge(fold_d, tile + 1)
                    out, before = p2[:, q % 2, :], p2[:, 1 - q % 2, :]
                    if q == 1 and not (isinstance(i, int) and i == 0):
                        dve.wait_ge(p2_full, i)
                    if q == 0:
                        nc.vector.tensor_scalar(out, total[:], 0.0, None, ALU.max).then_inc(p2_done, 1)
                    else:
                        dve.wait_ge(p2_done, tile)
                        nc.vector.scalar_tensor_tensor(out=out, in0=total[:], scalar=0.0, in1=before, op0=ALU.max,
                                                       op1=ALU.add).then_inc(p2_done, 1)

            def last_mlp():
                for c in range(1, C1, 2):
                    dve.wait_ge(h1_full, C1 + c + 1)
                    nc.vector.tensor_scalar(hid1_last[:, c, :], ya[c][:, 0:SB], bt1[:, c:c + 1], 0.0,
                                            ALU.add, ALU.max).then_inc(h1_last_v, 1)
                for c in range(1, C2, 2):
                    dve.wait_ge(h2_full, C2 + c + 1)
                    nc.vector.tensor_scalar(hid2[:, c, LAST], (x1_ps, yv[0])[c][:, 0:SB], bt2[:, c:c + 1], 0.0,
                                            ALU.add, ALU.max).then_inc(h2_last_v, 1)

            def step(i, first, ahead):
                for q in range(TILES):
                    for g, n in groups:
                        if KINDS[g] == "V":
                            k = V_GROUPS.index((g, n))
                            if ahead == 0 and q == TILES - 1:
                                if k == NV - 1:
                                    finish_tile(i, q, 0)
                                    finish_tile(i, q, 1)
                                mac_group(i, q, k, first, LAST_FINISH_AT)
                            else:
                                mac_group(i, q, k, first)
                        at = q * NG + g
                        if at == P1_AT:
                            sum_x1(i)
                        if ahead > 0 and at in PAIRS_AT:
                            multiply_pairs(i + 1, PAIRS_AT.index(at))
                        if ahead == 0 and at in (P1_LO_AT, P2_LO_AT):
                            k = (P1_LO_AT, P2_LO_AT).index(at)
                            dve.wait_ge(p_hi_set, k + 1)
                            nc.vector.tensor_tensor(p_lo[:, k, :], (p1_t, p2_t)[k][:, FRONT], p_hi[:, k, :],
                                                    ALU.subtract).then_inc(p_lo_set, 1)
                        if ahead == 0 and at in LOWS_AT:
                            k = LOWS_AT.index(at)
                            dve.wait_ge(h1_hi, k + 1)
                            nc.vector.tensor_tensor(hid1_lo[:, k, :], hid1[:, k % 2, :], hid1_hi[:, k, :],
                                                    ALU.subtract).then_inc(h1_lo, 1)
                        if ahead > 0 and at == LO_AT:
                            split_lo(i + 1, 0)
                if ahead > 0:
                    split_lo(i + 1, 1)

            dve.wait_ge(w1_in, 16 * 4)
            nc.vector.memset(w1r[0:FIELDS, 0, :], 0.0).then_inc(w1_fold, 1)
            dve.wait_ge(w1_fold, 1)
            nc.vector.tensor_tensor(w1s[:, 0:KT - 1, :], w1s[:, 0:KT - 1, :], w1r[:, 0:KT - 1, :], ALU.add)
            nc.vector.tensor_tensor(w1s[0:k_rows[-1], KT - 1, :], w1s[0:k_rows[-1], KT - 1, :],
                                    w1r[0:k_rows[-1], KT - 1, :], ALU.add).then_inc(w1_fold, 1)
            dve.wait_ge(w2_hi_set, 1)
            nc.vector.tensor_tensor(w2_lo[:], w2[:], w2_hi[:], ALU.subtract).then_inc(w2_lo_set, 1)
            dve.wait_ge(bias_in, 32)
            for t in range(KT):
                multiply_pairs(0, t)
            dve.wait_ge(mlp_hi_set, 1)
            nc.vector.tensor_tensor(wt1_lo[:], wt1[:], wt1_hi[:], ALU.subtract)
            nc.vector.tensor_tensor(wt1_dense_lo[:], wt1_dense[:], wt1_dense_hi[:], ALU.subtract)
            nc.vector.tensor_tensor(dense_lo[:], dense[:, FRONT], dense_hi[:], ALU.subtract)
            dve.wait_ge(mlp_hi_set, 2)
            nc.vector.tensor_tensor(wt2_lo[:], wt2[:], wt2_hi[:], ALU.subtract).then_inc(mlp_lo_set, 1)
            split_lo(0, 0)
            split_lo(0, 1)
            step(0, True, 1)
            with nc.vector.Fori(1, STEPS - 1) as i:
                step(i, False, 1)
            step(STEPS - 1, False, 0)
            for part in range(2, len(FINISH_AT)):
                finish_tile(STEPS - 1, TILES - 1, part)
            last_mlp()


def kernel(**inputs):
    import numpy as np
    import concourse.bacc as bacc
    from concourse import mybir as mb
    from concourse.bass_utils import run_bass_kernel_spmd

    fields = TABLES
    shifts = (fields + 1) // 2
    m = np.tile(np.arange(fields), shifts)
    far = (m + np.repeat(np.arange(shifts), fields)) % fields
    w1 = np.asarray(inputs["L0_rec_W1"])

    def columns(a):
        return np.asarray(a).reshape(-1, 128).T

    def by_partition(a):
        a = np.pad(a, ((0, 0), (0, -fields % 4))).reshape(-1, 32, (fields + 3) // 4, 4)
        return a.transpose(3, 1, 0, 2).reshape(128, -1)

    ids = np.asarray(inputs["ids"])
    tables = [np.asarray(inputs[f"tbl_{f}"]) for f in range(fields)]
    starts = np.array([sum(t.shape[0] for t in tables[:f]) for f in range(fields)], ids.dtype)

    arrays = {
        "dense_t": np.asarray(inputs["dense_ctx"]).T,
        "ids_t": by_partition(ids),
        "field_base": by_partition(np.broadcast_to(starts, ids.shape)),
        "table": np.concatenate(tables),
        "w1_fwd": w1[:, m, far].T,
        "w1_rev": w1[:, far, m].T,
        "b1": inputs["L0_rec_b1"],
        "w2_t": np.asarray(inputs["L0_rec_W2"]).transpose(1, 2, 0).reshape(128, -1),
        "b2": inputs["L0_rec_b2"],
        "w_top1": inputs["W_top1"], "b_top1": columns(inputs["b_top1"]),
        "w_top2": inputs["W_top2"], "b_top2": columns(inputs["b_top2"]),
        "w_top3": columns(inputs["W_top3"]),
    }
    arrays = {k: np.ascontiguousarray(a) for k, a in arrays.items()}
    batch = ids.shape[0]
    nc = bacc.Bacc("TRN2", target_bir_lowering=False, num_devices=1)
    aps = {k: nc.dram_tensor(k, a.shape, mb.dt.from_np(a.dtype), kind="ExternalInput").ap() for k, a in arrays.items()}
    y_out = nc.dram_tensor("y_out", (batch, 1), mb.dt.float32, kind="ExternalOutput").ap()
    build_tower(nc, y_out=y_out, **aps)
    result = run_bass_kernel_spmd(nc, [arrays], core_ids=[0])
    return result.results[0]["y_out"]
```
